# Optimizing a Trainium2 kernel written in Bass

```python
import numpy as np
import jax
import jax.numpy as jnp

def _softmax(x, axis=-1):
    return jax.nn.softmax(x, axis=axis)

def _gelu(x):
    return jax.nn.gelu(x, approximate=True)

def _silu(x):
    return jax.nn.silu(x)

def _sigmoid(x):
    return jax.nn.sigmoid(x)

def _layernorm(x, axis=-1, eps=1e-05):
    m = jnp.mean(x, axis=axis, keepdims=True)
    v = jnp.var(x, axis=axis, keepdims=True)
    return (x - m) / jnp.sqrt(v + eps)

def _scatter_add(tgt, idx, src, axis=0):
    return tgt.at[idx].add(src)

def _segment_sum(src, seg, n):
    return jax.ops.segment_sum(src, seg, n)
kernel_name = 'mk_seq_preln_d1_jaxref_r8_780300'

def setup_inputs(seed: int=0):
    np.random.seed(seed)
    _w = jnp.asarray

    def _L0_attn_setup():
        import jax, jax.numpy as jnp
        import numpy as np
        NUM_HEADS = 16

        def _l2_normalize_complex(z):
            n = jnp.sqrt(jnp.sum(jnp.abs(z) ** 2, axis=-1, keepdims=True))
            return z / n
        key = jax.random.key(seed)
        k1, k2, k3, k4 = jax.random.split(key, 4)
        B, S, D = (4, 512, 256)
        scale = 1.0 / np.sqrt(D)
        return {'x': jax.random.normal(k1, (B, S, D), dtype=jnp.float32), 'W_q': jax.random.normal(k2, (D, D), dtype=jnp.float32) * scale, 'W_kv': jax.random.normal(k3, (D, D), dtype=jnp.float32) * scale, 'W_o': jax.random.normal(k4, (D, D), dtype=jnp.float32) * scale}
    _L0_attn_in = _L0_attn_setup()

    def _L0_ffn_setup():
        import jax, jax.numpy as jnp
        import numpy as np
        B_, S, D = (2, 256, 256)
        F_ = 1024
        R = 16
        H = 16
        HD = D // H
        MOD_SCALE = 0.1
        EPS = 1e-06

        def _rmsnorm(x, w):
            v = jnp.mean(x * x, axis=-1, keepdims=True)
            return x * jax.lax.rsqrt(v + EPS) * w

        def _attention(x, Wq, Wk, Wv, Wo):
            b, s, d = x.shape
            q = (x @ Wq.T).reshape(b, s, H, HD)
            k = (x @ Wk.T).reshape(b, s, H, HD)
            v = (x @ Wv.T).reshape(b, s, H, HD)
            scores = jnp.einsum('bqhd,bkhd->bhqk', q, k) / np.sqrt(HD).astype(np.float32)
            causal = jnp.tril(jnp.ones((s, s), bool))
            scores = jnp.where(causal, scores, jnp.finfo(scores.dtype).min)
            probs = jax.nn.softmax(scores, axis=-1)
            out = jnp.einsum('bhqk,bkhd->bqhd', probs, v).reshape(b, s, d)
            return out @ Wo.T
        key = jax.random.key(seed)
        ks = jax.random.split(key, 12)
        sd = 0.02
        return {'hidden_states': jax.random.normal(ks[0], (B_, S, D), jnp.float32), 'ln1_w': jnp.ones((D,), jnp.float32), 'ln2_w': jnp.ones((D,), jnp.float32), 'Wq': jax.random.normal(ks[1], (D, D), jnp.float32) * sd, 'Wk': jax.random.normal(ks[2], (D, D), jnp.float32) * sd, 'Wv': jax.random.normal(ks[3], (D, D), jnp.float32) * sd, 'Wo': jax.random.normal(ks[4], (D, D), jnp.float32) * sd, 'A': jax.random.normal(ks[5], (D, R), jnp.float32) * (0.01 / np.sqrt(D)), 'B': jax.random.normal(ks[6], (R, F_), jnp.float32) * (0.01 / np.sqrt(R)), 'W_in_base': jax.random.normal(ks[7], (F_, D), jnp.float32) * sd, 'W_up_base': jax.random.normal(ks[8], (F_, D), jnp.float32) * sd, 'W_down': jax.random.normal(ks[9], (D, F_), jnp.float32) * sd}
    _L0_ffn_in = _L0_ffn_setup()
    _d = {'L0_attn_x': _L0_attn_in['x'], 'L0_attn_W_q': _L0_attn_in['W_q'], 'L0_attn_W_kv': _L0_attn_in['W_kv'], 'L0_attn_W_o': _L0_attn_in['W_o'], 'L0_ffn_ln1_w': _L0_ffn_in['ln1_w'], 'L0_ffn_ln2_w': _L0_ffn_in['ln2_w'], 'L0_ffn_Wq': _L0_ffn_in['Wq'], 'L0_ffn_Wk': _L0_ffn_in['Wk'], 'L0_ffn_Wv': _L0_ffn_in['Wv'], 'L0_ffn_Wo': _L0_ffn_in['Wo'], 'L0_ffn_A': _L0_ffn_in['A'], 'L0_ffn_B': _L0_ffn_in['B'], 'L0_ffn_W_in_base': _L0_ffn_in['W_in_base'], 'L0_ffn_W_up_base': _L0_ffn_in['W_up_base'], 'L0_ffn_W_down': _L0_ffn_in['W_down']}
    _x0 = _d['L0_attn_x']
    _d['L0_attn_x'] = jax.random.normal(jax.random.fold_in(jax.random.key(seed), 1), (1, 1024, 256), dtype=_x0.dtype)
    del _x0
    return _d

def reference(L0_attn_x, L0_attn_W_q, L0_attn_W_kv, L0_attn_W_o, L0_ffn_ln1_w, L0_ffn_ln2_w, L0_ffn_Wq, L0_ffn_Wk, L0_ffn_Wv, L0_ffn_Wo, L0_ffn_A, L0_ffn_B, L0_ffn_W_in_base, L0_ffn_W_up_base, L0_ffn_W_down):

    def _L0_attn_ref(x, W_q, W_kv, W_o):
        import jax, jax.numpy as jnp
        import numpy as np
        NUM_HEADS = 16

        def _l2_normalize_complex(z):
            n = jnp.sqrt(jnp.sum(jnp.abs(z) ** 2, axis=-1, keepdims=True))
            return z / n
        B, S, D = x.shape
        H = NUM_HEADS
        hd = D // H
        q = (x @ W_q.T).reshape(B, S, H, hd)
        kv = (x @ W_kv.T).reshape(B, S, H, hd)
        qf = jnp.fft.fft(q, axis=-1)
        kvf = jnp.fft.fft(kv, axis=-1)
        qf = _l2_normalize_complex(qf)
        kvf = _l2_normalize_complex(kvf)
        kvf = jnp.cumsum(kvf, axis=1)
        qv = qf * kvf
        values_hat = jnp.fft.ifft(qv, axis=-1).real.astype(x.dtype)
        values_hat = values_hat.reshape(B, S, D)
        return values_hat @ W_o.T

    def _L0_ffn_ref(hidden_states, ln1_w, ln2_w, Wq, Wk, Wv, Wo, A, B, W_in_base, W_up_base, W_down):
        import jax, jax.numpy as jnp
        import numpy as np
        B_, S, D = (2, 256, 256)
        F_ = 1024
        R = 16
        H = 16
        HD = D // H
        MOD_SCALE = 0.1
        EPS = 1e-06

        def _rmsnorm(x, w):
            v = jnp.mean(x * x, axis=-1, keepdims=True)
            return x * jax.lax.rsqrt(v + EPS) * w

        def _attention(x, Wq, Wk, Wv, Wo):
            b, s, d = x.shape
            q = (x @ Wq.T).reshape(b, s, H, HD)
            k = (x @ Wk.T).reshape(b, s, H, HD)
            v = (x @ Wv.T).reshape(b, s, H, HD)
            scores = jnp.einsum('bqhd,bkhd->bhqk', q, k) / np.sqrt(HD).astype(np.float32)
            causal = jnp.tril(jnp.ones((s, s), bool))
            scores = jnp.where(causal, scores, jnp.finfo(scores.dtype).min)
            probs = jax.nn.softmax(scores, axis=-1)
            out = jnp.einsum('bhqk,bkhd->bqhd', probs, v).reshape(b, s, d)
            return out @ Wo.T
        residual = hidden_states
        x = _rmsnorm(hidden_states, ln1_w)
        attn = _attention(x, Wq, Wk, Wv, Wo)
        mod = MOD_SCALE * jnp.tanh(attn @ A)
        h = _rmsnorm(residual, ln2_w)
        gate_pre = h @ W_in_base.T + mod * (h @ A) @ B
        gate = jax.nn.silu(gate_pre)
        up = h @ W_up_base.T
        mlp_out = gate * up @ W_down.T
        return residual + mlp_out
    x = L0_attn_x
    x = x + _L0_attn_ref(_layernorm(x, axis=-1), L0_attn_W_q, L0_attn_W_kv, L0_attn_W_o)
    x = x + _L0_ffn_ref(_layernorm(x, axis=-1), L0_ffn_ln1_w, L0_ffn_ln2_w, L0_ffn_Wq, L0_ffn_Wk, L0_ffn_Wv, L0_ffn_Wo, L0_ffn_A, L0_ffn_B, L0_ffn_W_in_base, L0_ffn_W_up_base, L0_ffn_W_down)
    return x

_drawn_inputs = setup_inputs


def setup_inputs(seed=0):
    import zlib

    import numpy as np

    out = dict(_drawn_inputs(seed))
    spreads = {'L0_ffn_ln1_w': (1.0, 0.6), 'L0_ffn_ln2_w': (1.0, 0.6)}
    factors = {'L0_ffn_Wq': 64.0,
     'L0_ffn_Wk': 64.0,
     'L0_ffn_Wv': 64.0,
     'L0_ffn_Wo': 64.0,
     'L0_ffn_A': 64.0,
     'L0_ffn_B': 64.0,
     'L0_ffn_W_in_base': 3.098,
     'L0_ffn_W_up_base': 3.048,
     'L0_ffn_W_down': 3.063}
    for name, (base, spread) in spreads.items():
        noise = np.random.default_rng([zlib.crc32(name.encode()), seed]).standard_normal(out[name].shape)
        drawn = base * np.exp(spread * noise) if base else spread * noise
        out[name] = jnp.asarray(drawn.astype(out[name].dtype))
    for name, factor in factors.items():
        out[name] = (out[name] * factor).astype(out[name].dtype)
    return out
```

```python
from contextlib import ExitStack

import concourse.bass as bass
import numpy as np
from concourse import mybir

P = 128
S = 1024
D = 256
H = 16
HD = D // H
F = 1024
R = 16
NT = S // P
NI = D // P
NF = F // P
BANK = 512
NC = S // BANK
HPH = P // HD
G = 4
NG = H // G
VW = 32
SLOTS = 6
KROWS = SLOTS * HD
MROWS = 3
LN_EPS = 1e-5
RMS_EPS = 1e-6
MOD_SCALE = 0.1
LOWEST = float(np.finfo(np.float32).min)
MASKED = -2.0 ** 127

ALU = mybir.AluOpType
ACT = mybir.ActivationFunctionType
AX = mybir.AxisListType
F32 = mybir.dt.float32
BF16 = mybir.dt.bfloat16

Q_PART = (0, 0, 0, 1, 1, 2)
K_PART = (0, 1, 2, 0, 1, 0)

C_DFT, C_IDFT, C_IDENT, C_TRI, C_ONES, C_LATER, C_BLOCK, C_MASK, C_END = (
    0, 128, 256, 384, 512, 640, 768, 776, 776 + S)


def constants():
    n, k = np.arange(HD)[:, None], np.arange(1, HD // 2)[None, :]
    angle = 2 * np.pi * n * k / HD
    dft = np.zeros((HD, HD))
    dft[:, 0] = 1 / np.sqrt(HD)
    dft[:, 1:HD // 2] = np.cos(angle) * np.sqrt(2 / HD)
    dft[:, HD // 2] = (-1.0) ** n[:, 0] / np.sqrt(HD)
    dft[:, HD // 2 + 1:] = -np.sin(angle) * np.sqrt(2 / HD)
    inv = np.zeros((HD, HD))
    inv[0] = 1 / HD
    inv[1:HD // 2] = np.cos(angle).T / HD
    inv[HD // 2] = (-1.0) ** n[:, 0] / HD
    inv[HD // 2 + 1:] = -np.sin(angle).T / HD
    c = np.zeros((P, C_END), np.float32)
    c[:, C_DFT:C_DFT + P] = np.kron(np.eye(HPH), dft)
    c[:, C_IDFT:C_IDFT + P] = np.kron(np.eye(HPH), inv.T)
    c[:, C_IDENT:C_IDENT + P] = np.eye(P)
    c[:, C_TRI:C_TRI + P] = np.triu(np.ones((P, P)))
    c[:, C_ONES:C_ONES + P] = 1
    c[:, C_LATER:C_LATER + P] = np.tril(np.ones((P, P)), -1) * MASKED
    c[:, C_BLOCK:C_BLOCK + HPH] = np.kron(np.eye(HPH), np.ones((HD, 1)))
    c[:, C_MASK + S - P:C_MASK + S] = np.where(np.triu(np.ones((P, P)), 1) > 0, LOWEST, 0)
    return c


def attention_steps():
    return [(c, b, max(0, b * P - c * BANK)) for c in range(NC) for b in range((c + 1) * BANK // P)]


def score_chunks():
    out = []
    for j in range(G):
        for i in range(NT):
            for c in range(i * P // BANK + 1):
                out.append((j, i, c, min(BANK, (i + 1) * P - c * BANK)))
    return out


STEPS = attention_steps()
CHUNKS = score_chunks()
NSTEP = len(STEPS)
NCHUNK = len(CHUNKS)
PER_HEAD = NCHUNK // G
PER_STEP = 5
RING = 3
USES = NCHUNK + 1
PRING = 6


SLOT_RUNS = (((0, 3, 0), (3, 2, 1), (5, 1, 2)), ((0, 3, 0), (3, 2, 0), (5, 1, 0)))
STACK_LOADS = sum(map(len, SLOT_RUNS))


class Counted:

    def __init__(self, sem):
        self.sem, self.value = sem, 0

    def mark(self, ins, by=1):
        ins.then_inc(self.sem, by)
        self.value += by
        return self.value


def seq_preln_kernel(nc, x, wq, wkv, wo_t, ln, fwq_t, fwk_t, fwv, fwo, a, b, win_t, wup_t,
                     wdown_t, consts, out):
    with ExitStack() as ctx:
        def sb(name, shape, dt=F32):
            return ctx.enter_context(nc.sbuf_tensor(name, shape, dt))

        def sem(name):
            return ctx.enter_context(nc.semaphore(name))

        class Region:

            def __init__(self, name, columns):
                self.all, self.at = sb(name, [P, columns]), 0

            def take(self, *shape, dt=F32):
                n = int(np.prod(shape)) * (1 if dt == F32 else 0.5)
                assert n == int(n) and self.at + n <= self.all.shape[1]
                v = self.all[:, self.at:self.at + int(n)]
                self.at += int(n)
                if dt != F32:
                    v = v.bitcast(dt)
                axes = " ".join(f"a{k}" for k in range(len(shape)))
                sizes = {f"a{k}": shape[k] for k in range(1, len(shape))}
                return v.rearrange(f"p ({axes}) -> p {axes}", **sizes) if len(shape) > 1 else v

            def again(self):
                self.at = 0
                return self

        spread = nc.dram_tensor("spread", (2, 3, NG, HD, G * S), BF16, kind="Internal").ap()

        region_a = Region("region_a", 6144)
        region_b = Region("region_b", 4096)
        region_c = Region("region_c", 6144)
        cst = sb("cst", [P, C_END])
        dft, idft = cst[:, C_DFT:C_DFT + P], cst[:, C_IDFT:C_IDFT + P]
        ident, tri = cst[:, C_IDENT:C_IDENT + P], cst[:, C_TRI:C_TRI + P]
        ones = cst[:, C_ONES:C_ONES + P]
        x_sb = region_b.take(NT, D)
        w_q = region_a.take(NI, D)
        w_kv = region_a.take(NI, D)
        w_o = region_a.take(NI, D)
        f_q = sb("f_q", [P, NI, D])
        f_k = sb("f_k", [P, NI, D])
        f_v = region_a.take(NI, D)
        f_o = region_a.take(NI, D)
        a_sb = sb("a_sb", [P, NI, R])
        lnw = sb("lnw", [P, 2, NI])
        spec_w = region_a.take(NI, 2 * D)
        spec_o = region_a.take(NI, D)
        m_sb = sb("m_sb", [P, NI, R])
        m_block = sb("m_block", [P, NI, HPH, R])
        w_u = sb("w_u", [P, NI, D + R])
        stats = sb("stats", [P, NT, 6])
        mv = sb("mv", [P, NT, 2])
        veps = sb("veps", [P, NT])
        std = sb("std", [P, NT])
        rstd = sb("rstd", [P, NT])
        xn = sb("xn", [P, 2, D])
        xn_t = sb("xn_t", [P, 2, D])
        sq = region_a.take(2, 2 * D)
        ss = sb("ss", [P, 2, 2 * H])
        norm = sb("norm", [P, 2, 2 * H])
        inv_norm = sb("inv_norm", [P, 2, 2 * H])
        qkn = region_a.take(2, 2 * D)
        kv_sum = region_b.take(NT, D)
        prod = sb("prod", [P, 2, D])
        cross = sb("cross", [P, 2, 2, H, HD // 2])
        prod_t = sb("prod_t", [P, 2, D])
        x1 = sb("x1", [P, 2, D])
        stats2 = sb("stats2", [P, 2, 6])
        mv2 = sb("mv2", [P, 2, 2])
        vars2 = sb("vars2", [P, 2, 2])
        stds2 = sb("stds2", [P, 2, 2])
        scales = sb("scales", [P, 2, 2])
        u = sb("u", [P, 2, D])
        h0 = sb("h0", [P, 2, D])
        base = sb("base", [P, NT, D])
        u_t = sb("u_t", [P, NI, S])
        part = [[region_c.take(3, S, dt=BF16) for hf in range(NI)] for w in range(2)]
        rest = sb("rest", [P, 2, BANK])
        q_stack = sb("q_stack", [P, H, S], BF16)
        k_stack = sb("k_stack", [P, H, S], BF16)
        vals = sb("vals", [P, NT, H, VW])
        ha = sb("ha", [P, NT, R])
        probs = region_a.again().take(PRING, 2, BANK)
        ident_b, later_b = sb("ident_b", [P, P], BF16), sb("later_b", [P, P], BF16)
        junk = sb("junk", [P, RING, BANK], BF16)
        mpart = sb("mpart", [P, 2, G, PER_HEAD])
        mfull = sb("mfull", [P, 2, G, NT])
        mrest = sb("mrest", [G * NT, 2, P])
        mparts = sb("mparts", [G * NT, 3, P], BF16)
        o_t = region_b.again().take(NG, S)
        linv = sb("linv", [P, 2, H])
        onorm = sb("onorm", [P, 2, H, R])
        attn_a = sb("attn_a", [P, 2, R])
        tanh_a = sb("tanh_a", [P, 2, R])
        mod_h = sb("mod_h", [P, 2, R])
        hidden = q_stack[:, :, :].bitcast(F32).rearrange("p (f a) n -> p f (a n)", f=NF)
        y_sb = k_stack[:, 0:NF, :].bitcast(F32).rearrange("p (t a) n -> p t (a n)", t=NT)[:, :, 0:D]
        w_down = k_stack[:, NF:2 * NF, :].bitcast(F32).rearrange("p f n -> p (f n)")[:, 0:NF * D].rearrange("p (f n) -> p f n", f=NF)
        region_c.again()
        w_in, w_up = region_c.take(NI, F), region_c.take(NI, F)
        b_sb, mod_t = region_c.take(F)[0:R, :], region_c.take(S)[0:R, :]
        gate = region_a.again().take(2, S)

        bank = [ctx.enter_context(nc.psum_tensor(f"bank{n}", [P, BANK], F32)) for n in range(4, 7)]
        pair = [ctx.enter_context(nc.psum_tensor(f"pair{n}", [P, 2, BANK], F32)) for n in range(2)]
        pv = ctx.enter_context(nc.psum_tensor("pv", [P, BANK], F32))
        b8 = [pair[0][:, 0, :], pair[0][:, 1, :], pair[1][:, 0, :], pair[1][:, 1, :],
              bank[0][:, :], bank[1][:, :], bank[2][:, :], pv[:, :]]

        ld_x, ld_cst, ld_spec, ld_attn, ld_ln, ld_mlp, ld_down = (
            sem(f"ld_{n}") for n in ("x", "cst", "spec", "attn", "ln", "mlp", "down"))
        parts_out = [sem(f"parts_out{n}") for n in range(NI)]
        stacked = [sem(f"stacked{n}") for n in range(NG)]
        max_landed = [sem(f"max_landed{n}") for n in range(NG)]
        stored = sem("stored")
        pe_spec, pe_speco, pe_m, pe_wu = sem("pe_spec"), sem("pe_speco"), sem("pe_m"), sem("pe_wu")
        pe_xt, pe_qk, pe_cum, pe_pt, pe_y, pe_ut = (sem(f"pe_{n}") for n in ("xt", "qk", "cum", "pt", "y", "ut"))
        pe_proj, pe_vals = sem("pe_proj"), sem("pe_vals")
        pe_chunk, pe_maxt, pe_pair, pe_pv, pe_pvlast = (
            sem(f"pe_{n}") for n in ("chunk", "maxt", "pair", "pv", "pvlast"))
        pe_ot, pe_modt, pe_gate, pe_up, pe_down = (sem(f"pe_{n}") for n in ("ot", "modt", "gate", "up", "down"))
        spec_ready, speco_ready, m_ready, mblock_ready, wu_ready = (
            sem(n) for n in ("spec_ready", "speco_ready", "m_ready", "mblock_ready", "wu_ready"))
        xn_ready, xt_ready, sq_ready, kvn_ready, qn_ready, sum_ready = (
            sem(n) for n in ("xn_ready", "xt_ready", "sq_ready", "kvn_ready", "qn_ready", "sum_ready"))
        prod_ready, pt_ready, x1_ready, u_ready, base_ready, ut_ready = (
            sem(n) for n in ("prod_ready", "pt_ready", "x1_ready", "u_ready", "base_ready", "ut_ready"))
        scaled_attn, scaled_mlp, pool_set = sem("scaled_attn"), sem("scaled_mlp"), sem("pool_set")
        part1, rest1, part2, part3 = (sem(n) for n in ("part1", "rest1", "part2", "part3"))
        vals_ready = sem("vals_ready")
        var_ready, std_ready, ss_ready, norm_ready, var2_ready, std2_ready = (
            sem(n) for n in ("var_ready", "std_ready", "ss_ready", "norm_ready", "var2_ready", "std2_ready"))
        ring_read, exp_ready, masks_ready, maxp_ready, ot_ready = (
            sem(n) for n in ("ring_read", "exp_ready", "masks_ready", "maxp_ready", "ot_ready"))
        lsum_read, attn_ready, tanh_ready, mod_ready, modt_ready = (
            sem(n) for n in ("lsum_read", "attn_ready", "tanh_ready", "mod_ready", "modt_ready"))
        maxf_ready = sem("maxf_ready")
        silu_ready, hid_ready, y_ready = sem("silu_ready"), sem("hid_ready"), sem("y_ready")
        dve_done = sem("dve_done")
        pool_done = sem("pool_done")
        block = ctx.enter_context(nc.Block())

        PSUM_T, PSUM_QK, PSUM_C, PSUM_PT, PSUM_Y, PSUM_UT = b8[0], (b8[1], b8[2]), b8[3], b8[4], b8[5], b8[6]

        @block.sync
        def _(sp):
            def rows(w):
                return w.rearrange("(n p) m -> p n m", p=P)

            sp.dma_start(x_sb[:, :, :], rows(x)).then_inc(ld_x, 16)
            sp.dma_start(cst[:, :], consts).then_inc(ld_cst, 16)
            for dst, src in ((w_q, wq), (w_kv, wkv), (w_o, wo_t)):
                sp.dma_start(dst[:, :, :], rows(src)).then_inc(ld_spec, 16)
            sp.dma_start(lnw[:, :, :], ln).then_inc(ld_ln, 16)
            for dst, src in ((f_q, fwq_t), (f_k, fwk_t), (f_v, fwv), (f_o, fwo), (a_sb, a)):
                sp.dma_start(dst[:, :, :], rows(src)).then_inc(ld_attn, 16)

            for hf in range(NI):
                for w in range(2):
                    for c in range(NC):
                        n = (hf * 2 + w) * NC + c
                        sp.wait_ge(part1, n + 1)
                        sp.wait_ge(part2, n + 1)
                        sp.wait_ge(part3, n + 1)
                        sp.dma_start(
                            spread.rearrange("w k g d (h n) -> w (g d h) k n", h=G)[
                                w, hf * P:(hf + 1) * P, :, c * BANK:(c + 1) * BANK],
                            part[w][hf][:, :, c * BANK:(c + 1) * BANK]).then_inc(parts_out[hf], 16)
                sp.wait_ge(parts_out[hf], 16 * 2 * NC)
                for g in range(hf * NG // NI, (hf + 1) * NG // NI):
                    for w, stack in enumerate((q_stack, k_stack)):
                        for slot, slots, part0 in SLOT_RUNS[w]:
                            src = spread[w, part0:part0 + (slots if w else 1), g]
                            sp.dma_start(stack[slot * HD:(slot + slots) * HD, g * G:(g + 1) * G, :],
                                         src.broadcast_to([slots, HD, G * S])).then_inc(stacked[g], 16)
            for g in range(NG):
                sp.wait_ge(maxp_ready, g + 1)
                for k in range(MROWS):
                    sp.dma_start(q_stack[KROWS + k:KROWS + k + 1, g * G:(g + 1) * G, :],
                                 mparts[:, k, :]).then_inc(max_landed[g], 16)
                if g == 1:
                    sp.wait_ge(parts_out[NI - 1], 16 * 2 * NC)
                    for dst, src in ((w_in, win_t), (w_up, wup_t)):
                        sp.dma_start(dst[:, :, :], rows(src)).then_inc(ld_mlp, 16)
                    sp.dma_start(b_sb, b).then_inc(ld_mlp, 16)
            sp.wait_ge(pe_pair, 2 * NG * NSTEP)
            sp.dma_start(w_down, rows(wdown_t)).then_inc(ld_down, 16)
            for t in range(NT):
                sp.wait_ge(y_ready, t + 1)
                sp.dma_start(out[t * P:(t + 1) * P, :], y_sb[:, t, :]).then_inc(stored, 16)
            sp.wait_ge(stored, 16 * NT)

        @block.tensor
        def _(pe):
            pe.wait_ge(ld_cst, 16)
            pe.wait_ge(ld_spec, 48)
            for i in range(NI):
                for w, src in enumerate((w_q, w_kv)):
                    for o in range(NI):
                        last = nc.tensor.matmul(b8[4 + i][:, w * D + o * P:w * D + (o + 1) * P],
                                                src[:, o, i * P:(i + 1) * P], dft, start=True, stop=True)
                last.then_inc(pe_spec, 1)
            for o in range(NI):
                last = nc.tensor.matmul(b8[6][:, o * D:(o + 1) * D], idft, w_o[:, o, :], start=True, stop=True)
            last.then_inc(pe_speco, 1)
            pe.wait_ge(ld_attn, 80)
            for j in range(NI):
                for o in range(NI):
                    last = nc.tensor.matmul(b8[7][:, j * R:(j + 1) * R], f_o[:, o, j * P:(j + 1) * P], a_sb[:, o, :],
                                            start=(o == 0), stop=(o == NI - 1))
            last.then_inc(pe_m, 1)

            def value_weights():
                pe.wait_ge(mblock_ready, 1)
                for i in range(NI):
                    for j in range(NI):
                        last = nc.tensor.matmul(b8[7][:, i * D + j * P:i * D + (j + 1) * P],
                                                f_v[:, j, i * P:(i + 1) * P], m_block[:, j, :, :],
                                                start=True, stop=True)
                last.then_inc(pe_wu, 1)

            def turn_x(t):
                pe.wait_ge(xn_ready, t + 1)
                if t >= 1:
                    pe.wait_ge(xt_ready, t)
                for i in range(NI):
                    last = nc.tensor.transpose(PSUM_T[:, i * P:(i + 1) * P], xn[:, t % 2, i * P:(i + 1) * P], ident)
                last.then_inc(pe_xt, 1)

            def project_qk(t):
                if t == 0:
                    pe.wait_ge(spec_ready, NI)
                pe.wait_ge(xt_ready, t + 1)
                if t >= 2:
                    pe.wait_ge(qn_ready, t - 1)
                for i in range(NI):
                    last = nc.tensor.matmul(PSUM_QK[t % 2], xn_t[:, t % 2, i * P:(i + 1) * P], spec_w[:, i, :],
                                            start=(i == 0), stop=(i == NI - 1))
                last.then_inc(pe_qk, 1)

            def cumulate(t):
                pe.wait_ge(kvn_ready, t + 1)
                if t >= 1:
                    pe.wait_ge(prod_ready, t)
                nc.tensor.matmul(PSUM_C[:, 0:D], tri, qkn[:, t % 2, D:2 * D], start=True,
                                 stop=(t == 0)).then_inc(pe_cum, 1)
                if t >= 1:
                    pe.wait_ge(sum_ready, t)
                    nc.tensor.matmul(PSUM_C[:, 0:D], ones, kv_sum[:, t, :], start=False, stop=True).then_inc(pe_cum, 1)

            def turn_prod(t):
                pe.wait_ge(prod_ready, t + 1)
                if t == 0:
                    pe.wait_ge(spec_ready, NI)
                if t >= 1:
                    pe.wait_ge(pt_ready, t)
                for i in range(NI):
                    last = nc.tensor.transpose(PSUM_PT[:, i * P:(i + 1) * P], prod[:, t % 2, i * P:(i + 1) * P], ident)
                last.then_inc(pe_pt, 1)

            def project_o(t):
                pe.wait_ge(pt_ready, t + 1)
                if t == 0:
                    pe.wait_ge(speco_ready, 1)
                if t >= 1:
                    pe.wait_ge(x1_ready, t)
                for i in range(NI):
                    last = nc.tensor.matmul(PSUM_Y[:, 0:D], prod_t[:, t % 2, i * P:(i + 1) * P], spec_o[:, i, :],
                                            start=(i == 0), stop=(i == NI - 1))
                last.then_inc(pe_y, 1)

            def turn_u(t):
                pe.wait_ge(u_ready, t + 1)
                if t >= 1:
                    pe.wait_ge(ut_ready, t)
                for i in range(NI):
                    last = nc.tensor.transpose(PSUM_UT[:, i * P:(i + 1) * P], u[:, t % 2, i * P:(i + 1) * P], ident)
                last.then_inc(pe_ut, 1)

            for n in range(NT + 4):
                if 0 <= n - 3 < NT:
                    project_o(n - 3)
                if n < NT:
                    turn_x(n)
                if 0 <= n - 4 < NT:
                    turn_u(n - 4)
                if n < NT:
                    project_qk(n)
                if n == 1:
                    value_weights()
                if 0 <= n - 2 < NT:
                    turn_prod(n - 2)
                if 0 <= n - 1 < NT:
                    cumulate(n - 1)

            pe.wait_ge(ut_ready, NT)
            pe.wait_ge(scaled_attn, 2 * NI)
            pe.wait_ge(prod_ready, NT)
            n = 0
            for hf in range(NI):
                for w in (f_q, f_k):
                    for c in range(NC):
                        if n >= 4:
                            pe.wait_ge(rest1, n - 3)
                        for i in range(NI):
                            last = nc.tensor.matmul(b8[n % 4], w[:, i, hf * P:(hf + 1) * P],
                                                    u_t[:, i, c * BANK:(c + 1) * BANK],
                                                    start=(i == 0), stop=(i == NI - 1))
                        last.then_inc(pe_proj, 1)
                        n += 1
            pe.wait_ge(wu_ready, 2 * NI)
            for t in range(NT):
                if t >= 3:
                    pe.wait_ge(vals_ready, 2 * (t - 2))
                for i in range(NI):
                    last = nc.tensor.matmul(b8[4 + t % 3][:, 0:D + R], u_t[:, i, t * P:(t + 1) * P], w_u[:, i, :],
                                            start=(i == 0), stop=(i == NI - 1))
                last.then_inc(pe_vals, 1)

            def chunk(g, n):
                j, i, c, keys = CHUNKS[n]
                h, use = g * G + j, g * USES + n
                if use >= RING:
                    pe.wait_ge(ring_read, use - RING + 1)
                nc.tensor.matmul(bank[use % RING][:, 0:keys], q_stack[0:KROWS, h, i * P:(i + 1) * P],
                                 k_stack[0:KROWS, h, c * BANK:c * BANK + keys],
                                 start=True, stop=True).then_inc(pe_chunk, 1)

            def turn_max(g):
                use = g * USES + NCHUNK
                pe.wait_ge(maxf_ready, g + 1)
                pe.wait_ge(ring_read, use - RING + 1)
                nc.tensor.transpose(bank[use % RING][0:G * NT, 0:P], mfull[:, g % 2, :, :], ident).then_inc(pe_maxt, 1)

            def score_pairs(g, n):
                c, b, q0 = STEPS[n]
                for d in range(2):
                    m = (g * NSTEP + n) * 2 + d
                    if m >= 2:
                        pe.wait_ge(exp_ready, m - 1)
                    for e in range(2):
                        h = g * G + 2 * d + e
                        last = nc.tensor.matmul(pair[m % 2][:, e, 0:BANK - q0],
                                                k_stack[0:KROWS + MROWS, h, b * P:(b + 1) * P],
                                                q_stack[0:KROWS + MROWS, h, c * BANK + q0:(c + 1) * BANK],
                                                start=True, stop=(b * P < c * BANK))
                        if b * P >= c * BANK:
                            last = nc.tensor.matmul(pair[m % 2][:, e, 0:P], ident_b[:, :], later_b[:, :],
                                                    start=False, stop=True)
                    last.then_inc(pe_pair, 1)

            def weigh(g, n):
                c, b, q0 = STEPS[n]
                m = (g * NSTEP + n) * 2
                pe.wait_ge(exp_ready, m + 2)
                if b == 0 and g * NC + c >= 1:
                    pe.wait_ge(ot_ready, g * NC + c)
                for j in range(G):
                    last = nc.tensor.matmul(pv[j * VW:(j + 1) * VW, q0:BANK], vals[:, b, g * G + j, :],
                                            probs[:, (m + j // 2) % PRING, j % 2, 0:BANK - q0],
                                            start=(b == 0), stop=(b == (c + 1) * BANK // P - 1),
                                            tile_position=(0, j * VW))
                last.then_inc(pe_pv, 1)

            pe.wait_ge(vals_ready, 2 * NT)
            pe.wait_ge(stacked[0], 16 * STACK_LOADS)
            for n in range(NCHUNK):
                chunk(0, n)
            turn_max(0)
            pe.wait_ge(masks_ready, 2)
            pe.wait_ge(pool_set, 2)
            pe.wait_ge(rest1, 2 * NI * NC)
            for g in range(NG):
                if g + 1 < NG:
                    pe.wait_ge(stacked[g + 1], 16 * STACK_LOADS)
                pe.wait_ge(max_landed[g], 16 * MROWS)
                at = 0
                for n in range(NSTEP):
                    score_pairs(g, n)
                    if g + 1 < NG:
                        for _ in range(PER_STEP):
                            if at < NCHUNK:
                                chunk(g + 1, at)
                                at += 1
                                if at == NCHUNK:
                                    turn_max(g + 1)
                    if n >= 1:
                        weigh(g, n - 1)
                weigh(g, NSTEP - 1)

            def turn_o(t):
                if t == 0:
                    pe.wait_ge(ot_ready, NG * NC)
                if t >= 2:
                    pe.wait_ge(lsum_read, t - 1)
                for g in range(NG):
                    last = nc.tensor.transpose(b8[t % 2][:, g * P:(g + 1) * P], o_t[:, g, t * P:(t + 1) * P], ident)
                last.then_inc(pe_ot, 1)

            def turn_mod(t):
                pe.wait_ge(mod_ready, t + 1)
                if t >= 2:
                    pe.wait_ge(modt_ready, t - 1)
                nc.tensor.transpose(b8[2 + t % 2][0:R, 0:P], mod_h[:, t % 2, :], ident).then_inc(pe_modt, 1)

            for t in range(NT):
                turn_o(t)
                if t >= 1:
                    turn_mod(t - 1)
            turn_mod(NT - 1)

            pe.wait_ge(scaled_mlp, 2 * NI)
            pe.wait_ge(modt_ready, NT)
            pe.wait_ge(lsum_read, NT)
            for f in range(NF):
                for c in range(NC):
                    n = NC * f + c
                    if n >= 4:
                        pe.wait_ge(silu_ready, n - 3)
                    for i in range(NI):
                        nc.tensor.matmul(b8[n % 4], w_in[:, i, f * P:(f + 1) * P], u_t[:, i, c * BANK:(c + 1) * BANK],
                                         start=(i == 0), stop=False)
                    nc.tensor.matmul(b8[n % 4], b_sb[:, f * P:(f + 1) * P], mod_t[:, c * BANK:(c + 1) * BANK],
                                     start=False, stop=True).then_inc(pe_gate, 1)
                    if n >= 4:
                        pe.wait_ge(hid_ready, n - 3)
                    for i in range(NI):
                        last = nc.tensor.matmul(b8[4 + n % 4], w_up[:, i, f * P:(f + 1) * P],
                                                u_t[:, i, c * BANK:(c + 1) * BANK],
                                                start=(i == 0), stop=(i == NI - 1))
                    last.then_inc(pe_up, 1)
            pe.wait_ge(ld_down, 16)
            pe.wait_ge(hid_ready, NF * NC)
            for t in range(NT):
                if t >= 4:
                    pe.wait_ge(y_ready, t - 3)
                for f in range(NF):
                    last = nc.tensor.matmul(b8[t % 4][:, 0:D], hidden[:, f, t * P:(t + 1) * P], w_down[:, f, :],
                                            start=(f == 0), stop=(f == NF - 1))
                last.then_inc(pe_down, 1)

        def read_pv(act, k):
            g, c = divmod(k, NC)
            done = g * NSTEP + sum(cc <= c for cc, _, _ in STEPS)
            act.wait_ge(pe_pv, done)
            nc.scalar.copy(o_t[:, g, c * BANK:(c + 1) * BANK], pv[:, :]).then_inc(ot_ready, 1)

        @block.scalar
        def _(act):
            for i in range(NI):
                act.wait_ge(pe_spec, i + 1)
                nc.scalar.copy(spec_w[:, i, :], b8[4 + i]).then_inc(spec_ready, 1)
            act.wait_ge(pe_speco, 1)
            nc.scalar.copy(spec_o[:, :, :], b8[6].rearrange("p (n m) -> p n m", n=NI)).then_inc(speco_ready, 1)
            act.wait_ge(pe_m, 1)
            nc.scalar.copy(m_sb[:, :, :], b8[7][:, 0:NI * R].rearrange("p (n r) -> p n r", n=NI)).then_inc(m_ready, 1)

            def read_xt(t):
                act.wait_ge(pe_xt, t + 1)
                if t >= 2:
                    act.wait_ge(pe_qk, t - 1)
                nc.scalar.copy(xn_t[:, t % 2, :], PSUM_T[:, 0:D]).then_inc(xt_ready, 1)

            def square(t):
                act.wait_ge(pe_qk, t + 1)
                if t >= 2:
                    act.wait_ge(ss_ready, t - 1)
                nc.scalar.activation(sq[:, t % 2, :], PSUM_QK[t % 2], ACT.Square).then_inc(sq_ready, 1)

            def read_pt(t):
                act.wait_ge(pe_pt, t + 1)
                if t >= 2:
                    act.wait_ge(pe_y, t - 1)
                nc.scalar.copy(prod_t[:, t % 2, :], PSUM_PT[:, 0:D]).then_inc(pt_ready, 1)

            def read_ut(t):
                act.wait_ge(pe_ut, t + 1)
                nc.scalar.copy(u_t[:, :, t * P:(t + 1) * P],
                               PSUM_UT[:, 0:D].rearrange("p (n m) -> p n m", n=NI)).then_inc(ut_ready, 1)

            act.wait_ge(var_ready, 1)
            nc.scalar.activation(std[:, :], veps[:, :], ACT.Sqrt).then_inc(std_ready, 1)
            for n in range(NT + 4):
                if 0 <= n - 1 < NT:
                    act.wait_ge(ss_ready, n)
                    nc.scalar.activation(norm[:, (n - 1) % 2, :], ss[:, (n - 1) % 2, :], ACT.Sqrt)\
                        .then_inc(norm_ready, 1)
                if n < NT:
                    read_xt(n)
                if 0 <= n - 4 < NT:
                    read_ut(n - 4)
                if n < NT:
                    square(n)
                if 0 <= n - 3 < NT:
                    act.wait_ge(var2_ready, n - 2)
                    nc.scalar.activation(stds2[:, (n - 3) % 2, :], vars2[:, (n - 3) % 2, :], ACT.Sqrt)\
                        .then_inc(std2_ready, 1)
                if n == 2:
                    act.wait_ge(pe_wu, 1)
                    act.wait_ge(ld_ln, 16)
                    for i in range(NI):
                        nc.scalar.activation(w_u[:, i, 0:D], b8[7][:, i * D:(i + 1) * D], ACT.Copy,
                                             scale=lnw[:, 0, i:i + 1]).then_inc(wu_ready, 1)
                        nc.scalar.activation(w_u[:, i, D:D + R], a_sb[:, i, :], ACT.Copy,
                                             scale=lnw[:, 1, i:i + 1]).then_inc(wu_ready, 1)
                if 0 <= n - 2 < NT:
                    read_pt(n - 2)
            n = 0
            for hf in range(NI):
                for w in range(2):
                    for c in range(NC):
                        act.wait_ge(pe_proj, n + 1)
                        nc.scalar.copy(part[w][hf][:, 0, c * BANK:(c + 1) * BANK], b8[n % 4]).then_inc(part1, 1)
                        n += 1
            for t in range(NT):
                act.wait_ge(pe_vals, t + 1)
                nc.scalar.copy(vals[:, t, :, 0:R], b8[4 + t % 3][:, 0:D].rearrange("p (h r) -> p h r", h=H))\
                    .then_inc(vals_ready, 1)
                nc.scalar.copy(ha[:, t, :], b8[4 + t % 3][:, D:D + R]).then_inc(vals_ready, 1)
            for g in range(NG):
                for n, (c, b, q0) in enumerate(STEPS):
                    for d in range(2):
                        m = (g * NSTEP + n) * 2 + d
                        act.wait_ge(pe_pair, m + 1)
                        if m >= PRING:
                            act.wait_ge(pe_pv, (m - PRING) // 2 + 1)
                        nc.scalar.activation(probs[:, m % PRING, :, 0:BANK - q0], pair[m % 2][:, :, 0:BANK - q0],
                                             ACT.Exp, scale=HD ** -0.5).then_inc(exp_ready, 1)
                    if b == 0 and g * NC + c >= 1:
                        read_pv(act, g * NC + c - 1)
            read_pv(act, NG * NC - 1)
            for t in range(NT):
                act.wait_ge(attn_ready, t + 1)
                nc.scalar.activation(tanh_a[:, t % 2, :], attn_a[:, t % 2, :], ACT.Tanh).then_inc(tanh_ready, 1)
                act.wait_ge(pe_modt, t + 1)
                nc.scalar.copy(mod_t[:, t * P:(t + 1) * P], b8[2 + t % 2][0:R, 0:P]).then_inc(modt_ready, 1)
            for n in range(NF * NC):
                act.wait_ge(pe_gate, n + 1)
                if n >= 4:
                    act.wait_ge(hid_ready, n - 3)
                nc.scalar.activation(gate[:, n // 2 % 2, n % 2 * BANK:(n % 2 + 1) * BANK], b8[n % 4], ACT.Silu)\
                    .then_inc(silu_ready, 1)

        @block.gpsimd
        def _(pool):
            nc.gpsimd.memset(k_stack[KROWS:KROWS + MROWS, :, :], -1.0).then_inc(pool_set, 1)
            pool.wait_ge(pool_set, 1)
            nc.gpsimd.memset(vals[:, :, :, R:VW], 1.0).then_inc(pool_set, 1)
            pool.wait_ge(ld_ln, 16)
            pool.wait_ge(ld_attn, 80)
            for w in (f_q, f_k):
                for i in range(NI):
                    nc.gpsimd.tensor_scalar(w[:, i, :], w[:, i, :], lnw[:, 0, i:i + 1], None, ALU.mult)\
                        .then_inc(scaled_attn, 1)
            for t in range(NT + 2):
                if t < NT - 1:
                    pool.wait_ge(kvn_ready, t + 1)
                    if t == 0:
                        nc.gpsimd.tensor_copy(kv_sum[:, 1, :], qkn[:, 0, D:2 * D]).then_inc(sum_ready, 1)
                    else:
                        pool.wait_ge(sum_ready, t)
                        nc.gpsimd.tensor_tensor(kv_sum[:, t + 1, :], kv_sum[:, t, :], qkn[:, t % 2, D:2 * D],
                                                ALU.add).then_inc(sum_ready, 1)
                if t >= 2:
                    k = t - 2
                    pool.wait_ge(u_ready, k + 1)
                    nc.gpsimd.tensor_scalar(h0[:, k % 2, :], x1[:, k % 2, :], mv2[:, k % 2, 0:1], scales[:, k % 2, 0:1],
                                            ALU.subtract, ALU.mult).then_inc(pool_done, 1)
                    pool.wait_ge(pool_done, k + 1)
                    nc.gpsimd.tensor_tensor(base[:, k, :], x1[:, k % 2, :], h0[:, k % 2, :], ALU.add)\
                        .then_inc(base_ready, 1)
            for n in range(2 * NI * NC):
                hf, w, c = n // (2 * NC), n // NC % 2, n % NC
                cols = slice(c * BANK, (c + 1) * BANK)
                pool.wait_ge(rest1, n + 1)
                pool.wait_ge(part2, n + 1)
                nc.gpsimd.tensor_tensor(part[w][hf][:, 2, cols], rest[:, n % 2, :], part[w][hf][:, 1, cols],
                                        ALU.subtract).then_inc(part3, 1)
            pool.wait_ge(ld_mlp, 48)
            for w in (w_in, w_up):
                for i in range(NI):
                    nc.gpsimd.tensor_scalar(w[:, i, :], w[:, i, :], lnw[:, 1, i:i + 1], None, ALU.mult)\
                        .then_inc(scaled_mlp, 1)

        @block.vector
        def _(dve):
            done = Counted(dve_done)

            def need(value):
                dve.wait_ge(dve_done, value)

            dve.wait_ge(ld_x, 16)
            for t in range(NT):
                v = done.mark(nc.vector.bn_stats(stats[:, t, :], x_sb[:, t, :]))
            need(v)
            for t in range(NT):
                v = done.mark(nc.vector.bn_aggr(mv[:, t, :], stats[:, t, :]))
            need(v)
            nc.vector.tensor_scalar(veps[:, :], mv[:, :, 1], LN_EPS, None, ALU.add).then_inc(var_ready, 1)
            dve.wait_ge(std_ready, 1)
            need(done.mark(nc.vector.reciprocal(rstd[:, :], std[:, :])))

            def normalize(t):
                if t >= 2:
                    dve.wait_ge(pe_xt, t - 1)
                nc.vector.tensor_scalar(xn[:, t % 2, :], x_sb[:, t, :], mv[:, t, 0:1], rstd[:, t:t + 1],
                                        ALU.subtract, ALU.mult).then_inc(xn_ready, 1)

            def spread_m():
                dve.wait_ge(m_ready, 1)
                dve.wait_ge(ld_cst, 16)
                for j in range(NI):
                    ins = nc.vector.tensor_tensor(
                        m_block[:, j, :, :], m_sb[:, j, :].unsqueeze(1).broadcast_to([P, HPH, R]),
                        cst[:, C_BLOCK:C_BLOCK + HPH].unsqueeze(2).broadcast_to([P, HPH, R]), ALU.mult)
                ins.then_inc(mblock_ready, 1)

            def energy(t):
                dve.wait_ge(sq_ready, t + 1)
                nc.vector.tensor_reduce(
                    ss[:, t % 2, :], sq[:, t % 2, :].rearrange("p (h s) -> p h s", s=HD), AX.X, ALU.add)\
                    .then_inc(ss_ready, 1)

            def unit(t):
                dve.wait_ge(norm_ready, t + 1)
                need(done.mark(nc.vector.reciprocal(inv_norm[:, t % 2, :], norm[:, t % 2, :])))
                if t >= 2:
                    dve.wait_ge(pe_cum, 2 * (t - 2) + 1)
                    dve.wait_ge(sum_ready, t - 1)
                for half, made in ((1, kvn_ready), (0, qn_ready)):
                    nc.vector.tensor_tensor(
                        qkn[:, t % 2, half * D:(half + 1) * D].rearrange("p (h s) -> p h s", s=HD),
                        PSUM_QK[t % 2][:, half * D:(half + 1) * D].rearrange("p (h s) -> p h s", s=HD),
                        inv_norm[:, t % 2, half * H:(half + 1) * H].unsqueeze(2).broadcast_to([P, H, HD]),
                        ALU.mult).then_inc(made, 1)

            def multiply(t):
                dve.wait_ge(pe_cum, 2 * t + 1)
                dve.wait_ge(qn_ready, t + 1)
                if t >= 2:
                    dve.wait_ge(pe_pt, t - 1)
                q = qkn[:, t % 2, 0:D].rearrange("p (h a s) -> p h a s", a=2, s=HD // 2)
                c = PSUM_C[:, 0:D].rearrange("p (h a s) -> p h a s", a=2, s=HD // 2)
                o = prod[:, t % 2, :].rearrange("p (h a s) -> p h a s", a=2, s=HD // 2)
                v = done.mark(nc.vector.tensor_tensor(prod[:, t % 2, :], qkn[:, t % 2, 0:D], PSUM_C[:, 0:D], ALU.mult))
                for e in range(2):
                    w = done.mark(nc.vector.tensor_tensor(cross[:, t % 2, e, :, :], q[:, :, e, :], c[:, :, 1 - e, :],
                                                          ALU.mult))
                need(v)
                v = done.mark(nc.vector.tensor_tensor(o[:, :, 0, 1:], o[:, :, 0, 1:], o[:, :, 1, 1:], ALU.subtract))
                need(v)
                nc.vector.tensor_tensor(o[:, :, 1, 1:], cross[:, t % 2, 0, :, 1:], cross[:, t % 2, 1, :, 1:],
                                        ALU.add).then_inc(prod_ready, 1)

            def norms(t):
                p = t % 2
                dve.wait_ge(pe_y, t + 1)
                if t >= 2:
                    dve.wait_ge(base_ready, t - 1)
                    dve.wait_ge(pe_ut, t - 1)
                nc.vector.tensor_tensor(x1[:, p, :], x_sb[:, t, :], PSUM_Y[:, 0:D], ALU.add).then_inc(x1_ready, 1)
                dve.wait_ge(x1_ready, t + 1)
                need(done.mark(nc.vector.bn_stats(stats2[:, p, :], x1[:, p, :])))
                need(done.mark(nc.vector.bn_aggr(mv2[:, p, :], stats2[:, p, :])))
                v = done.mark(nc.vector.tensor_scalar(vars2[:, p, 0:1], mv2[:, p, 1:2], LN_EPS, None, ALU.add))
                nc.vector.tensor_scalar(vars2[:, p, 1:2], mv2[:, p, 1:2], 1 + RMS_EPS, LN_EPS * RMS_EPS, ALU.mult,
                                        ALU.add).then_inc(var2_ready, 1)

            def norm_u(t):
                p = t % 2
                dve.wait_ge(std2_ready, t + 1)
                need(done.mark(nc.vector.reciprocal(scales[:, p, :], stds2[:, p, :])))
                nc.vector.tensor_scalar(u[:, p, :], x1[:, p, :], mv2[:, p, 0:1], scales[:, p, 1:2], ALU.subtract, ALU.mult)\
                    .then_inc(u_ready, 1)

            normalize(0)
            for n in range(NT + 4):
                if 0 <= n - 1 < NT:
                    energy(n - 1)
                if 0 <= n - 2 < NT:
                    multiply(n - 2)
                if 0 <= n - 1 < NT:
                    unit(n - 1)
                if 0 <= n - 3 < NT:
                    norms(n - 3)
                if n + 1 < NT:
                    normalize(n + 1)
                if n == 0:
                    spread_m()
                if n == 5:
                    for dst, src in ((ident_b, ident), (later_b, cst[:, C_LATER:C_LATER + P])):
                        nc.vector.tensor_copy(dst[:, :], src).then_inc(masks_ready, 1)
                if 0 <= n - 3 < NT:
                    norm_u(n - 3)

            for n in range(2 * NI * NC):
                hf, w, c = n // (2 * NC), n // NC % 2, n % NC
                dve.wait_ge(part1, n + 1)
                if n >= 2:
                    dve.wait_ge(part3, n - 1)
                nc.vector.tensor_tensor(rest[:, n % 2, :], b8[n % 4], part[w][hf][:, 0, c * BANK:(c + 1) * BANK],
                                        ALU.subtract).then_inc(rest1, 1)
                dve.wait_ge(rest1, n + 1)
                nc.vector.tensor_copy(part[w][hf][:, 1, c * BANK:(c + 1) * BANK], rest[:, n % 2, :]).then_inc(part2, 1)

            def maxima(g, n):
                j, i, c, keys = CHUNKS[n]
                use = g * USES + n
                dve.wait_ge(pe_chunk, g * NCHUNK + n + 1)
                if use >= RING:
                    dve.wait_ge(ring_read, use - RING + 1)
                mask = C_MASK + S - (i + 1) * P + c * BANK
                nc.vector.tensor_tensor_reduce(junk[:, use % RING, 0:keys], bank[use % RING][:, 0:keys], cst[:, mask:mask + keys],
                                               1.0, LOWEST, ALU.add, ALU.max,
                                               mpart[:, g % 2, j, n % PER_HEAD:n % PER_HEAD + 1]).then_inc(ring_read, 1)

            def merge(g):
                p, near = g % 2, BANK // P
                dve.wait_ge(ring_read, g * USES + NCHUNK)
                if g >= 2:
                    dve.wait_ge(pe_maxt, g - 1)
                need(done.mark(nc.vector.tensor_copy(mfull[:, p, :, 0:near], mpart[:, p, :, 0:near])))
                far = mpart[:, p, :, near:].rearrange("p j (i c) -> p j i c", c=NC)
                nc.vector.tensor_tensor(mfull[:, p, :, near:], far[:, :, :, 0], far[:, :, :, 1], ALU.max)\
                    .then_inc(maxf_ready, 1)

            def split_max(g):
                use = g * USES + NCHUNK
                src = bank[use % RING][0:G * NT, 0:P]
                dve.wait_ge(pe_maxt, g + 1)
                if g >= 1:
                    dve.wait_ge(max_landed[g - 1], 16 * MROWS)
                need(done.mark(nc.vector.tensor_copy(mparts[:, 0, :], src)))
                nc.vector.tensor_tensor(mrest[:, 0, :], src, mparts[:, 0, :], ALU.subtract).then_inc(ring_read, 1)
                dve.wait_ge(ring_read, use + 1)
                need(done.mark(nc.vector.tensor_copy(mparts[:, 1, :], mrest[:, 0, :])))
                nc.vector.tensor_tensor(mparts[:, 2, :], mrest[:, 0, :], mparts[:, 1, :], ALU.subtract)\
                    .then_inc(maxp_ready, 1)

            for g in range(NG):
                for n in range(NCHUNK):
                    maxima(g, n)
                merge(g)
                split_max(g)

            def by_token(t):
                o = b8[t % 2].rearrange("p (h v) -> p h v", v=VW)
                dve.wait_ge(pe_ot, t + 1)
                need(done.mark(nc.vector.reciprocal(linv[:, t % 2, :], o[:, :, R])))
                nc.vector.tensor_tensor(onorm[:, t % 2, :, :], o[:, :, 0:R],
                                        linv[:, t % 2, :].unsqueeze(2).broadcast_to([P, H, R]), ALU.mult)\
                    .then_inc(lsum_read, 1)
                dve.wait_ge(lsum_read, t + 1)
                if t >= 2:
                    dve.wait_ge(tanh_ready, t - 1)
                nc.vector.tensor_reduce(attn_a[:, t % 2, :], onorm[:, t % 2, :, :].rearrange("p h r -> p r h"),
                                        AX.X, ALU.add).then_inc(attn_ready, 1)

            def modulate(t):
                dve.wait_ge(tanh_ready, t + 1)
                if t >= 2:
                    dve.wait_ge(pe_modt, t - 1)
                nc.vector.scalar_tensor_tensor(mod_h[:, t % 2, :], tanh_a[:, t % 2, :], MOD_SCALE, ha[:, t, :],
                                               ALU.mult, ALU.mult).then_inc(mod_ready, 1)

            dve.wait_ge(vals_ready, 2 * NT)
            for t in range(NT):
                by_token(t)
                if t >= 1:
                    modulate(t - 1)
            modulate(NT - 1)

            for n in range(NF * NC):
                dve.wait_ge(silu_ready, n + 1)
                dve.wait_ge(pe_up, n + 1)
                nc.vector.tensor_tensor(hidden[:, n // 2, n % 2 * BANK:(n % 2 + 1) * BANK],
                                        gate[:, n // 2 % 2, n % 2 * BANK:(n % 2 + 1) * BANK], b8[4 + n % 4], ALU.mult)\
                    .then_inc(hid_ready, 1)
            dve.wait_ge(base_ready, NT)
            for t in range(NT):
                dve.wait_ge(pe_down, t + 1)
                nc.vector.tensor_tensor(y_sb[:, t, :], b8[t % 4][:, 0:D], base[:, t, :], ALU.add).then_inc(y_ready, 1)


def by_row_of_head(w):
    return np.asarray(w).reshape(NG, G, HD, D).transpose(3, 0, 2, 1).reshape(D, D)


def kernel(L0_attn_x, L0_attn_W_q, L0_attn_W_kv, L0_attn_W_o, L0_ffn_ln1_w, L0_ffn_ln2_w, L0_ffn_Wq, L0_ffn_Wk,
           L0_ffn_Wv, L0_ffn_Wo, L0_ffn_A, L0_ffn_B, L0_ffn_W_in_base, L0_ffn_W_up_base, L0_ffn_W_down):
    from concourse import bacc
    from concourse.bass_utils import run_bass_kernel_spmd

    nc = bacc.Bacc("TRN2", target_bir_lowering=False, num_devices=1)
    arrays = {
        "x": np.asarray(L0_attn_x).reshape(S, D),
        "wq": L0_attn_W_q,
        "wkv": L0_attn_W_kv,
        "wo_t": np.asarray(L0_attn_W_o).T,
        "ln": np.stack([np.asarray(w).reshape(NI, P) for w in (L0_ffn_ln1_w, L0_ffn_ln2_w)]).transpose(2, 0, 1),
        "fwq_t": by_row_of_head(L0_ffn_Wq),
        "fwk_t": by_row_of_head(L0_ffn_Wk),
        "fwv": L0_ffn_Wv,
        "fwo": L0_ffn_Wo,
        "a": L0_ffn_A,
        "b": L0_ffn_B,
        "win_t": np.asarray(L0_ffn_W_in_base).T,
        "wup_t": np.asarray(L0_ffn_W_up_base).T,
        "wdown_t": np.asarray(L0_ffn_W_down).T,
        "consts": constants(),
    }
    arrays = {f"in_{k}": np.ascontiguousarray(v) for k, v in arrays.items()}
    args = [nc.dram_tensor(k, v.shape, mybir.dt.from_np(v.dtype), kind="ExternalInput").ap() for k, v in arrays.items()]
    out = nc.dram_tensor("out", (S, D), F32, kind="ExternalOutput").ap()
    seq_preln_kernel(nc, *args, out)
    r = run_bass_kernel_spmd(nc, [arrays], core_ids=[0])
    return r.results[0]["out"].reshape(1, S, D)
```

```python
from contextlib import ExitStack

import concourse.bass as bass
import numpy as np
from concourse import mybir

P = 128
S = 1024
D = 256
H = 16
HD = D // H
F = 1024
R = 16
NT = S // P
NI = D // P
NF = F // P
BANK = 512
NC = S // BANK
HPH = P // HD
G = 4
NG = H // G
VW = 32
SLOTS = 6
KROWS = SLOTS * HD
MROWS = 3
LN_EPS = 1e-5
RMS_EPS = 1e-6
MOD_SCALE = 0.1
LOWEST = float(np.finfo(np.float32).min)
ALIGNED = 32
MASKED = -2.0 ** 127

ALU = mybir.AluOpType
ACT = mybir.ActivationFunctionType
AX = mybir.AxisListType
F32 = mybir.dt.float32
BF16 = mybir.dt.bfloat16
F32R = mybir.dt.float32r

Q_PART = (0, 0, 0, 1, 1, 2)
K_PART = (0, 1, 2, 0, 1, 0)

C_DFT, C_IDFT, C_IDENT, C_TRI, C_ONES, C_LATER, C_BLOCK, C_MASK, C_END = (
    0, 128, 256, 384, 512, 640, 768, 776, 776 + S)


def constants():
    n, k = np.arange(HD)[:, None], np.arange(1, HD // 2)[None, :]
    angle = 2 * np.pi * n * k / HD
    dft = np.zeros((HD, HD))
    dft[:, 0] = 1 / np.sqrt(HD)
    dft[:, 1:HD // 2] = np.cos(angle) * np.sqrt(2 / HD)
    dft[:, HD // 2] = (-1.0) ** n[:, 0] / np.sqrt(HD)
    dft[:, HD // 2 + 1:] = -np.sin(angle) * np.sqrt(2 / HD)
    inv = np.zeros((HD, HD))
    inv[0] = 1 / HD
    inv[1:HD // 2] = np.cos(angle).T / HD
    inv[HD // 2] = (-1.0) ** n[:, 0] / HD
    inv[HD // 2 + 1:] = -np.sin(angle).T / HD
    c = np.zeros((P, C_END), np.float32)
    c[:, C_DFT:C_DFT + P] = np.kron(np.eye(HPH), dft)
    c[:, C_IDFT:C_IDFT + P] = np.kron(np.eye(HPH), inv.T)
    c[:, C_IDENT:C_IDENT + P] = np.eye(P)
    c[:, C_TRI:C_TRI + P] = np.triu(np.ones((P, P)))
    c[:, C_ONES:C_ONES + P] = 1
    c[:, C_LATER:C_LATER + P] = np.tril(np.ones((P, P)), -1) * MASKED
    c[:, C_BLOCK:C_BLOCK + HPH] = np.kron(np.eye(HPH), np.ones((HD, 1)))
    c[:, C_MASK + S - P:C_MASK + S] = np.where(np.triu(np.ones((P, P)), 1) > 0, LOWEST, 0)
    return c


def attention_steps():
    return [(c, b, max(0, b * P - c * BANK)) for c in range(NC) for b in range((c + 1) * BANK // P)]


def score_chunks(c):
    tiles = BANK // P
    return [(j, i, k, min(BANK, (i + 1) * P - k * BANK))
            for j in range(G) for i in range(c * tiles, (c + 1) * tiles) for k in range(c + 1)]


STEPS = attention_steps()
NSTEP = len(STEPS)
CHUNKS = [score_chunks(c) for c in range(NC)]
NU = NG * NC
QT = BANK // P
RING = 3
PRING = 6
TURN_AFTER = 3
FIRST_LEAD, LEAD = 9000, 17000


def ring_uses():
    uses = []
    for u in range(NU):
        for n in range(len(CHUNKS[u % NC])):
            uses.append((u, n))
            if u >= 1 and n == TURN_AFTER - 1:
                uses.append((u - 1, None))
    return uses + [(NU - 1, None)]


def uses_before_pairs():
    before, k, used, scored = [], 0, 0, 0
    for g in range(NG):
        for c, b, q0 in STEPS:
            for d in range(2):
                lead = min(LEAD, FIRST_LEAD + 2 * scored)
                while k < len(USES) and (used < scored + lead or UNIT_READY[g * NC + c] > k):
                    u, n = USES[k]
                    used += CHUNKS[u % NC][n][3] if n is not None else P
                    k += 1
                before.append(k)
                scored += 2 * (BANK - q0)
    return before


USES = ring_uses()
UNIT_READY = [USES.index((u, None)) + 1 for u in range(NU)]
USES_BEFORE = uses_before_pairs()


PROJECTIONS = [(hf, c, w) for hf in range(NI) for c in range(NC) for w in range(2)]
FIRST_TURN = NG * NSTEP - 6
EARLY = 2

SLOT_RUNS = (((0, 3, 0), (3, 2, 1), (5, 1, 2)), ((0, 3, 0), (3, 2, 0), (5, 1, 0)))
STACK_LOADS = sum(map(len, SLOT_RUNS))


class Counted:

    def __init__(self, sem):
        self.sem, self.value = sem, 0

    def mark(self, ins, by=1):
        ins.then_inc(self.sem, by)
        self.value += by
        return self.value


def seq_preln_kernel(nc, x, wq, wkv, wo_t, ln, fwq_t, fwk_t, fwv, fwo, a, b, win_t, wup_t,
                     wdown_t, consts, out):
    with ExitStack() as ctx:
        def sb(name, shape, dt=F32):
            return ctx.enter_context(nc.sbuf_tensor(name, shape, dt))

        def sem(name):
            return ctx.enter_context(nc.semaphore(name))

        def next_base():
            return -(-nc.sbuf_base // ALIGNED) * ALIGNED

        class Region:

            def __init__(self, name, columns):
                self.base = next_base()
                self.all, self.at = sb(name, [P, columns]), 0

            def take(self, *shape, dt=F32):
                n = int(np.prod(shape)) * (1 if dt == F32 else 0.5)
                assert n == int(n) and self.at + n <= self.all.shape[1]
                v = self.all[:, self.at:self.at + int(n)]
                self.at += int(n)
                if dt != F32:
                    v = v.bitcast(dt)
                axes = " ".join(f"a{k}" for k in range(len(shape)))
                sizes = {f"a{k}": shape[k] for k in range(1, len(shape))}
                return v.rearrange(f"p ({axes}) -> p {axes}", **sizes) if len(shape) > 1 else v

            def again(self):
                self.at = 0
                return self

        def placed(name, shape, base, offset=0):
            return nc.alloc_sbuf_tensor_at(name, shape, F32R, offset=base + offset)

        spread = nc.dram_tensor("spread", (2, 3, NG, HD, G * S), BF16, kind="Internal").ap()

        region_a = Region("region_a", 6144)
        region_b = Region("region_b", 4096)
        region_c = Region("region_c", 6144)
        region_d = Region("region_d", 4096)
        region_e = Region("region_e", 1024)
        cst = sb("cst", [P, C_END])
        dft, idft = cst[:, C_DFT:C_DFT + P], cst[:, C_IDFT:C_IDFT + P]
        ident, tri = cst[:, C_IDENT:C_IDENT + P], cst[:, C_TRI:C_TRI + P]
        ones = cst[:, C_ONES:C_ONES + P]
        x_sb = region_b.take(NT, D)
        w_q = region_a.take(NI, D)
        w_kv = region_a.take(NI, D)
        w_o = region_a.take(NI, D)
        f_q = region_e.take(NI, D)
        f_k = region_e.take(NI, D)
        f_v = region_a.take(NI, D)
        f_o = region_a.take(NI, D)
        a_sb = sb("a_sb", [P, NI, R])
        lnw = sb("lnw", [P, 2, NI])
        spec_w = region_a.take(NI, 2 * D)
        spec_o = region_a.take(NI, D)
        m_sb = sb("m_sb", [P, NI, R])
        m_block = sb("m_block", [P, NI, HPH, R])
        w_u = sb("w_u", [P, NI, D + R])
        stats = sb("stats", [P, NT, 6])
        mv = sb("mv", [P, NT, 2])
        veps = sb("veps", [P, NT])
        std = sb("std", [P, NT])
        rstd = sb("rstd", [P, NT])
        xn = region_d.take(2, D)
        xn_t = region_d.take(2, D)
        sq = region_a.take(2, 2 * D)
        ss = sb("ss", [P, 2, 2 * H])
        norm = sb("norm", [P, 2, 2 * H])
        inv_norm = sb("inv_norm", [P, 2, 2 * H])
        qkn = region_a.take(2, 2 * D)
        kv_sum = region_b.take(NT, D)
        prod = region_d.take(2, D)
        cross = region_d.take(2, 2, H, HD // 2)
        prod_t = region_d.take(2, D)
        x1 = region_d.take(2, D)
        stats2 = sb("stats2", [P, 2, 6])
        mv2 = sb("mv2", [P, 2, 2])
        vars2 = sb("vars2", [P, 2, 2])
        stds2 = sb("stds2", [P, 2, 2])
        scales = sb("scales", [P, 2, 2])
        u = region_d.take(2, D)
        h0 = region_d.take(2, D)
        base = sb("base", [P, NT, D])
        ut_base, u_t = next_base(), sb("u_t", [P, NI, S])
        part = [[region_c.take(3, S, dt=BF16) for hf in range(NI)] for w in range(2)]
        rest = sb("rest", [P, 2, BANK])
        q_base, q_stack = next_base(), sb("q_stack", [P, H, S], BF16)
        k_base, k_stack = next_base(), sb("k_stack", [P, H, S], BF16)
        vals_base, vals = next_base(), sb("vals", [P, NT, H, VW])
        ha = sb("ha", [P, NT, R])
        probs = region_a.again().take(PRING, 2, BANK)
        ident_b, later_b = sb("ident_b", [P, P], BF16), sb("later_b", [P, P], BF16)
        junk = sb("junk", [P, RING, BANK], BF16)
        mpart = sb("mpart", [P, 2, NC, QT, G])
        mrest = sb("mrest", [P, QT, G])
        mparts = sb("mparts", [P, 2, QT, MROWS, G], BF16)
        mrows = sb("mrows", [MROWS * G, 2, BANK], BF16)
        o_t = region_b.again().take(NG, S)
        linv = sb("linv", [P, 2, H])
        onorm = sb("onorm", [P, 2, H, R])
        attn_a = sb("attn_a", [P, NT, R])
        tanh_a = sb("tanh_a", [P, NT, R])
        mod_h = sb("mod_h", [P, NT, R])
        region_e.again()
        mod_rest = onorm[:, 0, 0:NT, :]
        mod_parts = region_e.take(NT, SLOTS, R, dt=BF16)
        mod_t = region_e.take(S, dt=BF16)[0:KROWS, :]
        region_d.again()
        b_sb, b_rest = region_d.take(F)[0:R, :], region_d.take(F)[0:R, :]
        b_parts = region_d.take(3, F, dt=BF16)[0:R, :, :]
        b_stack = region_d.take(F, dt=BF16)[0:KROWS, :]

        region_c.again()
        w_in, w_up, w_down = region_c.take(NI, F), region_c.take(NI, F), region_c.take(NF, D)
        W = 4 * NI * F
        w_in_lo = placed("w_in_lo", [P, NI, F], region_c.base)
        w_up_lo = placed("w_up_lo", [P, NI, F], region_c.base, W)
        w_down_lo = placed("w_down_lo", [P, NF, D], region_c.base, 2 * W)
        u_lo = placed("u_lo", [P, NI, S], ut_base)
        group_bytes = 2 * G * S
        w_in_hi = placed("w_in_hi", [P, NI, F], q_base)
        w_up_hi = placed("w_up_hi", [P, NI, F], k_base)
        u_hi = placed("u_hi", [P, NI, S], q_base, group_bytes)
        w_down_hi = placed("w_down_hi", [P, NF, D], k_base, group_bytes)
        H_BYTES = 4 * 2 * S
        places = [(region_a.base, 0), (region_a.base, H_BYTES), (region_a.base, 2 * H_BYTES),
                  (q_base, 2 * group_bytes), (q_base, 3 * group_bytes),
                  (k_base, 2 * group_bytes), (k_base, 3 * group_bytes), (vals_base, 0)]
        hidden = [placed(f"hidden{f}", [P, 2, S], *places[f]) for f in range(NF)]
        gate = vals[:, NT // 2:, :, :].rearrange("p t h v -> p (t h v)").rearrange("p (n m) -> p n m", m=BANK)
        y_sb = region_b.again().take(NT, D)

        bank = [ctx.enter_context(nc.psum_tensor(f"bank{n}", [P, BANK], F32)) for n in range(4, 7)]
        pair = [ctx.enter_context(nc.psum_tensor(f"pair{n}", [P, 2, BANK], F32)) for n in range(2)]
        pv = ctx.enter_context(nc.psum_tensor("pv", [P, BANK], F32))
        b8 = [pair[0][:, 0, :], pair[0][:, 1, :], pair[1][:, 0, :], pair[1][:, 1, :],
              bank[0][:, :], bank[1][:, :], bank[2][:, :], pv[:, :]]

        ld_x, ld_cst, ld_spec, ld_attn, ld_ln, ld_mlp, ld_b, b_stacked = (
            sem(f"ld_{n}") for n in ("x", "cst", "spec", "attn", "ln", "mlp", "b", "b_stacked"))
        parts_out = [sem(f"parts_out{n}") for n in range(NI)]
        stacked = [sem(f"stacked{n}") for n in range(NG)]
        max_landed = [sem(f"max_landed{n}") for n in range(NU)]
        stored = sem("stored")
        pe_spec, pe_speco, pe_m, pe_wu = sem("pe_spec"), sem("pe_speco"), sem("pe_m"), sem("pe_wu")
        pe_xt, pe_qk, pe_cum, pe_pt, pe_y, pe_ut = (sem(f"pe_{n}") for n in ("xt", "qk", "cum", "pt", "y", "ut"))
        pe_proj, pe_vals = sem("pe_proj"), sem("pe_vals")
        pe_ring, pe_pair, pe_pv = sem("pe_ring"), sem("pe_pair"), sem("pe_pv")
        pe_ot, pe_modt, pe_gate, pe_up, pe_down = (sem(f"pe_{n}") for n in ("ot", "modt", "gate", "up", "down"))
        spec_ready, speco_ready, m_ready, mblock_ready, wu_ready = (
            sem(n) for n in ("spec_ready", "speco_ready", "m_ready", "mblock_ready", "wu_ready"))
        xn_ready, xt_ready, sq_ready, kvn_ready, qn_ready, sum_ready = (
            sem(n) for n in ("xn_ready", "xt_ready", "sq_ready", "kvn_ready", "qn_ready", "sum_ready"))
        prod_ready, pt_ready, x1_ready, u_ready, base_ready, ut_ready = (
            sem(n) for n in ("prod_ready", "pt_ready", "x1_ready", "u_ready", "base_ready", "ut_ready"))
        scaled_attn, scaled_mlp, pool_set = sem("scaled_attn"), sem("scaled_mlp"), sem("pool_set")
        part1, rest1, part2, part3 = (sem(n) for n in ("part1", "rest1", "part2", "part3"))
        vals_ready = sem("vals_ready")
        var_ready, std_ready, ss_ready, norm_ready, var2_ready, std2_ready = (
            sem(n) for n in ("var_ready", "std_ready", "ss_ready", "norm_ready", "var2_ready", "std2_ready"))
        ring_read, exp_ready, masks_ready, maxp_ready, ot_ready = (
            sem(n) for n in ("ring_read", "exp_ready", "masks_ready", "maxp_ready", "ot_ready"))
        lsum_read, attn_ready, tanh_ready, mod_ready, modt_ready = (
            sem(n) for n in ("lsum_read", "attn_ready", "tanh_ready", "mod_ready", "modt_ready"))
        bparts_ready, wsplit_ready, mparts_ready = sem("bparts_ready"), sem("wsplit_ready"), sem("mparts_ready")
        silu_ready, gated, high_ready, hid_ready, y_ready = (
            sem(n) for n in ("silu_ready", "gated", "high_ready", "hid_ready", "y_ready"))
        dve_done = sem("dve_done")
        pool_done, pool_steps = sem("pool_done"), sem("pool_steps")
        block = ctx.enter_context(nc.Block())

        PSUM_T, PSUM_QK, PSUM_C, PSUM_PT, PSUM_Y, PSUM_UT = b8[0], (b8[1], b8[2]), b8[3], b8[4], b8[5], b8[6]

        @block.sync
        def _(sp):
            def rows(w):
                return w.rearrange("(n p) m -> p n m", p=P)

            sp.dma_start(x_sb[:, :, :], rows(x)).then_inc(ld_x, 16)
            sp.dma_start(cst[:, :], consts).then_inc(ld_cst, 16)
            for dst, src in ((w_q, wq), (w_kv, wkv), (w_o, wo_t)):
                sp.dma_start(dst[:, :, :], rows(src)).then_inc(ld_spec, 16)
            sp.dma_start(lnw[:, :, :], ln).then_inc(ld_ln, 16)
            for dst, src in ((f_q, fwq_t), (f_k, fwk_t), (f_v, fwv), (f_o, fwo), (a_sb, a)):
                sp.dma_start(dst[:, :, :], rows(src)).then_inc(ld_attn, 16)

            def load_stacks(g):
                for w, stack in enumerate((q_stack, k_stack)):
                    for slot, slots, part0 in SLOT_RUNS[w]:
                        src = spread[w, part0:part0 + (slots if w else 1), g]
                        sp.dma_start(stack[slot * HD:(slot + slots) * HD, g * G:(g + 1) * G, :],
                                     src.broadcast_to([slots, HD, G * S])).then_inc(stacked[g], 16)

            for n, (hf, c, w) in enumerate(PROJECTIONS):
                sp.wait_ge(part1, n + 1)
                sp.wait_ge(part2, n + 1)
                sp.wait_ge(part3, n + 1)
                sp.dma_start(
                    spread.rearrange("w k g d (h n) -> w (g d h) k n", h=G)[
                        w, hf * P:(hf + 1) * P, :, c * BANK:(c + 1) * BANK],
                    part[w][hf][:, :, c * BANK:(c + 1) * BANK]).then_inc(parts_out[hf], 16)
                if n == 2 * NC - 1:
                    sp.wait_ge(parts_out[0], 16 * 2 * NC)
                    load_stacks(0)
                    load_stacks(1)
            for un in range(NU):
                g, c = divmod(un, NC)
                sp.wait_ge(ring_read, UNIT_READY[un])
                sp.dma_start(q_stack[KROWS:KROWS + MROWS, g * G:(g + 1) * G, c * BANK:(c + 1) * BANK],
                             mrows[:, un % 2, :]).then_inc(max_landed[un], 16)
                if un < 2:
                    sp.wait_ge(parts_out[1], 16 * 2 * NC)
                    load_stacks(NG // NI + un)
                if un == 1:
                    sp.wait_ge(base_ready, NT)
                    sp.wait_ge(pe_ut, NT)
                    sp.dma_start(b_sb, b).then_inc(ld_b, 16)
                    for dst, src in ((w_in, win_t), (w_up, wup_t), (w_down, wdown_t)):
                        sp.dma_start(dst[:, :, :], rows(src)).then_inc(ld_mlp, 16)
                if un == 4:
                    sp.wait_ge(bparts_ready, 2)
                    for slot in range(SLOTS):
                        sp.dma_start(b_stack[slot * R:(slot + 1) * R, :], b_parts[:, K_PART[slot], :])\
                            .then_inc(b_stacked, 16)
            for t in range(NT):
                sp.wait_ge(y_ready, t + 1)
                sp.dma_start(out[t * P:(t + 1) * P, :], y_sb[:, t, :]).then_inc(stored, 16)
            sp.wait_ge(stored, 16 * NT)

        @block.tensor
        def _(pe):
            pe.wait_ge(ld_cst, 16)
            pe.wait_ge(ld_spec, 48)
            for i in range(NI):
                for w, src in enumerate((w_q, w_kv)):
                    for o in range(NI):
                        last = nc.tensor.matmul(b8[4 + i][:, w * D + o * P:w * D + (o + 1) * P],
                                                src[:, o, i * P:(i + 1) * P], dft, start=True, stop=True)
                last.then_inc(pe_spec, 1)
            for o in range(NI):
                last = nc.tensor.matmul(b8[6][:, o * D:(o + 1) * D], idft, w_o[:, o, :], start=True, stop=True)
            last.then_inc(pe_speco, 1)
            pe.wait_ge(ld_attn, 80)
            for j in range(NI):
                for o in range(NI):
                    last = nc.tensor.matmul(b8[7][:, j * R:(j + 1) * R], f_o[:, o, j * P:(j + 1) * P], a_sb[:, o, :],
                                            start=(o == 0), stop=(o == NI - 1))
            last.then_inc(pe_m, 1)

            def value_weights():
                pe.wait_ge(mblock_ready, 1)
                for i in range(NI):
                    for j in range(NI):
                        last = nc.tensor.matmul(b8[7][:, i * D + j * P:i * D + (j + 1) * P],
                                                f_v[:, j, i * P:(i + 1) * P], m_block[:, j, :, :],
                                                start=True, stop=True)
                last.then_inc(pe_wu, 1)

            def turn_x(t):
                pe.wait_ge(xn_ready, t + 1)
                if t >= 1:
                    pe.wait_ge(xt_ready, t)
                for i in range(NI):
                    last = nc.tensor.transpose(PSUM_T[:, i * P:(i + 1) * P], xn[:, t % 2, i * P:(i + 1) * P], ident)
                last.then_inc(pe_xt, 1)

            def project_qk(t):
                if t == 0:
                    pe.wait_ge(spec_ready, NI)
                pe.wait_ge(xt_ready, t + 1)
                if t >= 2:
                    pe.wait_ge(qn_ready, t - 1)
                for i in range(NI):
                    last = nc.tensor.matmul(PSUM_QK[t % 2], xn_t[:, t % 2, i * P:(i + 1) * P], spec_w[:, i, :],
                                            start=(i == 0), stop=(i == NI - 1))
                last.then_inc(pe_qk, 1)

            def cumulate(t):
                pe.wait_ge(kvn_ready, t + 1)
                if t >= 1:
                    pe.wait_ge(prod_ready, t)
                nc.tensor.matmul(PSUM_C[:, 0:D], tri, qkn[:, t % 2, D:2 * D], start=True,
                                 stop=(t == 0)).then_inc(pe_cum, 1)
                if t >= 1:
                    pe.wait_ge(sum_ready, t)
                    nc.tensor.matmul(PSUM_C[:, 0:D], ones, kv_sum[:, t, :], start=False, stop=True).then_inc(pe_cum, 1)

            def turn_prod(t):
                pe.wait_ge(prod_ready, t + 1)
                if t == 0:
                    pe.wait_ge(spec_ready, NI)
                if t >= 1:
                    pe.wait_ge(pt_ready, t)
                for i in range(NI):
                    last = nc.tensor.transpose(PSUM_PT[:, i * P:(i + 1) * P], prod[:, t % 2, i * P:(i + 1) * P], ident)
                last.then_inc(pe_pt, 1)

            def project_o(t):
                pe.wait_ge(pt_ready, t + 1)
                if t == 0:
                    pe.wait_ge(speco_ready, 1)
                if t >= 1:
                    pe.wait_ge(x1_ready, t)
                for i in range(NI):
                    last = nc.tensor.matmul(PSUM_Y[:, 0:D], prod_t[:, t % 2, i * P:(i + 1) * P], spec_o[:, i, :],
                                            start=(i == 0), stop=(i == NI - 1))
                last.then_inc(pe_y, 1)

            def turn_u(t):
                pe.wait_ge(u_ready, t + 1)
                if t >= 1:
                    pe.wait_ge(ut_ready, t)
                for i in range(NI):
                    last = nc.tensor.transpose(PSUM_UT[:, i * P:(i + 1) * P], u[:, t % 2, i * P:(i + 1) * P], ident)
                last.then_inc(pe_ut, 1)

            def project_part(n):
                hf, c, w = PROJECTIONS[n]
                weights = (f_q, f_k)[w]
                if n == 0:
                    pe.wait_ge(scaled_attn, 2 * NI)
                    pe.wait_ge(xt_ready, NT)
                elif n < 3:
                    pe.wait_ge(qn_ready, NT - 2 + n)
                elif n == 3:
                    pe.wait_ge(prod_ready, NT)
                else:
                    pe.wait_ge(rest1, n - 3)
                pe.wait_ge(ut_ready, (c + 1) * BANK // P)
                for i in range(NI):
                    last = nc.tensor.matmul(b8[n % 4], weights[:, i, hf * P:(hf + 1) * P],
                                            u_t[:, i, c * BANK:(c + 1) * BANK],
                                            start=(i == 0), stop=(i == NI - 1))
                last.then_inc(pe_proj, 1)

            for n in range(NT + 4):
                if 0 <= n - 3 < NT:
                    project_o(n - 3)
                if n < NT:
                    turn_x(n)
                if 0 <= n - 4 < NT:
                    turn_u(n - 4)
                if n < NT:
                    project_qk(n)
                if n == 1:
                    value_weights()
                if 0 <= n - 2 < NT:
                    turn_prod(n - 2)
                if 0 <= n - 1 < NT:
                    cumulate(n - 1)
                if 0 <= n - (NT + 4 - 1 - EARLY) < EARLY:
                    project_part(n - (NT + 4 - 1 - EARLY))

            for n in range(EARLY, 2 * NC):
                project_part(n)
            pe.wait_ge(wu_ready, 2 * NI)
            for t in range(NT):
                if t >= 3:
                    pe.wait_ge(vals_ready, 2 * (t - 2))
                for i in range(NI):
                    last = nc.tensor.matmul(b8[4 + t % 3][:, 0:D + R], u_t[:, i, t * P:(t + 1) * P], w_u[:, i, :],
                                            start=(i == 0), stop=(i == NI - 1))
                last.then_inc(pe_vals, 1)
            for n in range(2 * NC, 2 * NC * NI):
                project_part(n)

            def use_ring(use):
                u, n = USES[use]
                if use >= RING:
                    pe.wait_ge(ring_read, use - RING + 1)
                if n is None:
                    pe.wait_ge(maxp_ready, u + 1)
                    for i in range(QT):
                        last = nc.tensor.matmul(bank[use % RING][0:MROWS * G, i * P:(i + 1) * P],
                                                mparts[:, u % 2, i, :, :], ident_b[:, :], start=True, stop=True)
                    last.then_inc(pe_ring, 1)
                    return
                j, i, k, keys = CHUNKS[u % NC][n]
                h = u // NC * G + j
                if u % NC == 0 and n == 0:
                    pe.wait_ge(stacked[u // NC], 16 * STACK_LOADS)
                nc.tensor.matmul(bank[use % RING][:, 0:keys], q_stack[0:KROWS, h, i * P:(i + 1) * P],
                                 k_stack[0:KROWS, h, k * BANK:k * BANK + keys],
                                 start=True, stop=True).then_inc(pe_ring, 1)

            def score_pair(m):
                (g, n), d = divmod(m // 2, NSTEP), m % 2
                c, b, q0 = STEPS[n]
                if d == 0 and b == 0:
                    pe.wait_ge(max_landed[g * NC + c], 16)
                if m >= 2:
                    pe.wait_ge(exp_ready, m - 1)
                for e in range(2):
                    h = g * G + 2 * d + e
                    last = nc.tensor.matmul(pair[m % 2][:, e, 0:BANK - q0],
                                            k_stack[0:KROWS + MROWS, h, b * P:(b + 1) * P],
                                            q_stack[0:KROWS + MROWS, h, c * BANK + q0:(c + 1) * BANK],
                                            start=True, stop=(b * P < c * BANK))
                    if b * P >= c * BANK:
                        last = nc.tensor.matmul(pair[m % 2][:, e, 0:P], ident_b[:, :], later_b[:, :],
                                                start=False, stop=True)
                last.then_inc(pe_pair, 1)

            def weigh(g, n):
                c, b, q0 = STEPS[n]
                m = (g * NSTEP + n) * 2
                pe.wait_ge(exp_ready, m + 2)
                if b == 0 and g * NC + c >= 1:
                    pe.wait_ge(ot_ready, g * NC + c)
                for j in range(G):
                    last = nc.tensor.matmul(pv[j * VW:(j + 1) * VW, q0:BANK], vals[:, b, g * G + j, :],
                                            probs[:, (m + j // 2) % PRING, j % 2, 0:BANK - q0],
                                            start=(b == 0), stop=(b == (c + 1) * BANK // P - 1),
                                            tile_position=(0, j * VW))
                last.then_inc(pe_pv, 1)

            pe.wait_ge(vals_ready, 2 * NT)
            def turn_o(t):
                pe.wait_ge(ot_ready, NC * (NG - 1) + t // QT + 1)
                if t == 0:
                    pe.wait_ge(ring_read, len(USES))
                if t >= 2:
                    pe.wait_ge(lsum_read, t - 1)
                for g in range(NG):
                    last = nc.tensor.transpose(bank[t % 2][:, g * P:(g + 1) * P], o_t[:, g, t * P:(t + 1) * P], ident)
                last.then_inc(pe_ot, 1)

            def turn_mod(c):
                pe.wait_ge(mparts_ready, c + 1)
                if c >= 1:
                    pe.wait_ge(modt_ready, c)
                for t in range(QT):
                    last = nc.tensor.matmul(bank[2][0:KROWS, t * P:(t + 1) * P], mod_parts[:, c * QT + t, :, :],
                                            ident_b[:, :], start=True, stop=True)
                last.then_inc(pe_modt, 1)

            pe.wait_ge(masks_ready, 2)
            at = 0
            for s in range(NG * NSTEP):
                for m in (2 * s, 2 * s + 1):
                    for use in range(at, USES_BEFORE[m]):
                        use_ring(use)
                    at = USES_BEFORE[m]
                    if m == 0:
                        pe.wait_ge(pool_set, 2)
                        pe.wait_ge(rest1, 2 * NI * NC)
                    score_pair(m)
                if s >= 1:
                    weigh(*divmod(s - 1, NSTEP))
                if 0 <= s - FIRST_TURN < QT:
                    turn_o(s - FIRST_TURN)
            weigh(NG - 1, NSTEP - 1)
            turn_mod(0)

            def product(out, w_hi, w_lo, f, c, stop):
                cols, toks = slice(f * P, (f + 1) * P), slice(c * BANK, (c + 1) * BANK)
                passes = [(w_hi, u_hi), (w_lo, u_hi), (w_hi, u_lo)]
                for i in range(NI):
                    for k, (w, act) in enumerate(passes):
                        last = nc.tensor.matmul(out, w[:, i, cols], act[:, i, toks], start=(i == 0 and k == 0),
                                                stop=(stop and i == NI - 1 and k == len(passes) - 1))
                return last

            def gate_product(n):
                c, f = divmod(n, NF)
                if n >= 2:
                    pe.wait_ge(silu_ready, n - 1)
                product(b8[n % 2], w_in_hi, w_in_lo, f, c, False)
                pe.wait_ge(modt_ready, c + 1)
                nc.tensor.matmul(b8[n % 2], b_stack[:, f * P:(f + 1) * P], mod_t[:, c * BANK:(c + 1) * BANK],
                                 start=False, stop=True).then_inc(pe_gate, 1)

            def up_product(n):
                c, f = divmod(n, NF)
                if n >= 2:
                    pe.wait_ge(gated, n - 1)
                product(b8[2 + n % 2], w_up_hi, w_up_lo, f, c, True).then_inc(pe_up, 1)

            pe.wait_ge(wsplit_ready, 3)
            pe.wait_ge(b_stacked, 16 * SLOTS)
            pe.wait_ge(exp_ready, 2 * NG * NSTEP)
            for n in range(NF * NC):
                up_product(n)
                if n == 0:
                    turn_o(QT)
                    turn_o(QT + 1)
                gate_product(n)
                if n == 0:
                    turn_o(QT + 2)
                    turn_o(QT + 3)
                if n == 2:
                    turn_mod(1)
            pe.wait_ge(wsplit_ready, 4)
            pe.wait_ge(modt_ready, NC)
            for t in range(NT):
                pe.wait_ge(hid_ready, (t // QT + 1) * NF)
                if t >= 4:
                    pe.wait_ge(y_ready, t - 3)
                toks = slice(t * P, (t + 1) * P)
                for f in range(NF):
                    for k, (part_h, w) in enumerate(((0, w_down_hi), (1, w_down_hi), (0, w_down_lo))):
                        last = nc.tensor.matmul(b8[4 + t % 4][:, 0:D], hidden[f][:, part_h, toks], w[:, f, :],
                                                start=(f == 0 and k == 0), stop=(f == NF - 1 and k == 2))
                last.then_inc(pe_down, 1)

        def read_pv(act, k):
            g, c = divmod(k, NC)
            done = g * NSTEP + sum(cc <= c for cc, _, _ in STEPS)
            act.wait_ge(pe_pv, done)
            nc.scalar.copy(o_t[:, g, c * BANK:(c + 1) * BANK], pv[:, :]).then_inc(ot_ready, 1)

        @block.scalar
        def _(act):
            for i in range(NI):
                act.wait_ge(pe_spec, i + 1)
                nc.scalar.copy(spec_w[:, i, :], b8[4 + i]).then_inc(spec_ready, 1)
            act.wait_ge(pe_speco, 1)
            nc.scalar.copy(spec_o[:, :, :], b8[6].rearrange("p (n m) -> p n m", n=NI)).then_inc(speco_ready, 1)
            act.wait_ge(pe_m, 1)
            nc.scalar.copy(m_sb[:, :, :], b8[7][:, 0:NI * R].rearrange("p (n r) -> p n r", n=NI)).then_inc(m_ready, 1)

            def read_xt(t):
                act.wait_ge(pe_xt, t + 1)
                if t >= 2:
                    act.wait_ge(pe_qk, t - 1)
                nc.scalar.copy(xn_t[:, t % 2, :], PSUM_T[:, 0:D]).then_inc(xt_ready, 1)

            def square(t):
                act.wait_ge(pe_qk, t + 1)
                if t >= 2:
                    act.wait_ge(ss_ready, t - 1)
                nc.scalar.activation(sq[:, t % 2, :], PSUM_QK[t % 2], ACT.Square).then_inc(sq_ready, 1)

            def read_pt(t):
                act.wait_ge(pe_pt, t + 1)
                if t >= 2:
                    act.wait_ge(pe_y, t - 1)
                nc.scalar.copy(prod_t[:, t % 2, :], PSUM_PT[:, 0:D]).then_inc(pt_ready, 1)

            def read_ut(t):
                act.wait_ge(pe_ut, t + 1)
                nc.scalar.copy(u_t[:, :, t * P:(t + 1) * P],
                               PSUM_UT[:, 0:D].rearrange("p (n m) -> p n m", n=NI)).then_inc(ut_ready, 1)

            def first_part(n):
                hf, c, w = PROJECTIONS[n]
                act.wait_ge(pe_proj, n + 1)
                nc.scalar.copy(part[w][hf][:, 0, c * BANK:(c + 1) * BANK], b8[n % 4]).then_inc(part1, 1)

            act.wait_ge(var_ready, 1)
            nc.scalar.activation(std[:, :], veps[:, :], ACT.Sqrt).then_inc(std_ready, 1)
            for n in range(NT + 4):
                if 0 <= n - 1 < NT:
                    act.wait_ge(ss_ready, n)
                    nc.scalar.activation(norm[:, (n - 1) % 2, :], ss[:, (n - 1) % 2, :], ACT.Sqrt)\
                        .then_inc(norm_ready, 1)
                if n < NT:
                    read_xt(n)
                if 0 <= n - 4 < NT:
                    read_ut(n - 4)
                if n < NT:
                    square(n)
                if 0 <= n - 3 < NT:
                    act.wait_ge(var2_ready, n - 2)
                    nc.scalar.activation(stds2[:, (n - 3) % 2, :], vars2[:, (n - 3) % 2, :], ACT.Sqrt)\
                        .then_inc(std2_ready, 1)
                if n == 2:
                    act.wait_ge(pe_wu, 1)
                    act.wait_ge(ld_ln, 16)
                    for i in range(NI):
                        nc.scalar.activation(w_u[:, i, 0:D], b8[7][:, i * D:(i + 1) * D], ACT.Copy,
                                             scale=lnw[:, 0, i:i + 1]).then_inc(wu_ready, 1)
                        nc.scalar.activation(w_u[:, i, D:D + R], a_sb[:, i, :], ACT.Copy,
                                             scale=lnw[:, 1, i:i + 1]).then_inc(wu_ready, 1)
                if 0 <= n - 2 < NT:
                    read_pt(n - 2)
                if n == NT + 2:
                    first_part(0)
            for n in range(1, 2 * NC):
                first_part(n)
            for t in range(NT):
                act.wait_ge(pe_vals, t + 1)
                nc.scalar.copy(vals[:, t, :, 0:R], b8[4 + t % 3][:, 0:D].rearrange("p (h r) -> p h r", h=H))\
                    .then_inc(vals_ready, 1)
                nc.scalar.copy(ha[:, t, :], b8[4 + t % 3][:, D:D + R]).then_inc(vals_ready, 1)
            for n in range(2 * NC, 2 * NC * NI):
                first_part(n)
            def tanh(c):
                toks = slice(c * QT, (c + 1) * QT)
                act.wait_ge(attn_ready, (c + 1) * QT)
                nc.scalar.activation(tanh_a[:, toks, :], attn_a[:, toks, :], ACT.Tanh).then_inc(tanh_ready, 1)

            def read_modt(c):
                act.wait_ge(pe_modt, c + 1)
                nc.scalar.copy(mod_t[:, c * BANK:(c + 1) * BANK], bank[2][0:KROWS, :]).then_inc(modt_ready, 1)

            def high(n):
                c, f = divmod(n, NF)
                act.wait_ge(gated, n + 1)
                nc.scalar.copy(hidden[f][:, 0, c * BANK:(c + 1) * BANK], gate[:, n % 4, :]).then_inc(high_ready, 1)

            for g in range(NG):
                for n, (c, b, q0) in enumerate(STEPS):
                    for d in range(2):
                        m = (g * NSTEP + n) * 2 + d
                        act.wait_ge(pe_pair, m + 1)
                        if m >= PRING:
                            act.wait_ge(pe_pv, (m - PRING) // 2 + 1)
                        nc.scalar.activation(probs[:, m % PRING, :, 0:BANK - q0], pair[m % 2][:, :, 0:BANK - q0],
                                             ACT.Exp, scale=HD ** -0.5).then_inc(exp_ready, 1)
                    if b == 0 and g * NC + c >= 1:
                        read_pv(act, g * NC + c - 1)
                    if g * NSTEP + n == NG * NSTEP - 1:
                        tanh(0)
                        read_modt(0)
            read_pv(act, NG * NC - 1)
            tanh(1)
            for n in range(NF * NC):
                act.wait_ge(pe_gate, n + 1)
                if n >= 4:
                    act.wait_ge(hid_ready, n - 3)
                nc.scalar.activation(gate[:, n % 4, :], b8[n % 2], ACT.Silu).then_inc(silu_ready, 1)
                if n >= 1:
                    high(n - 1)
                if n == 1:
                    read_modt(1)
            high(NF * NC - 1)

        @block.gpsimd
        def _(pool):
            nc.gpsimd.memset(k_stack[KROWS:KROWS + MROWS, :, :], -1.0).then_inc(pool_set, 1)
            pool.wait_ge(pool_set, 1)
            nc.gpsimd.memset(vals[:, :, :, R:VW], 1.0).then_inc(pool_set, 1)
            pool.wait_ge(ld_ln, 16)
            pool.wait_ge(ld_attn, 80)
            for w in (f_q, f_k):
                for i in range(NI):
                    nc.gpsimd.tensor_scalar(w[:, i, :], w[:, i, :], lnw[:, 0, i:i + 1], None, ALU.mult)\
                        .then_inc(scaled_attn, 1)
            for t in range(NT + 2):
                if t < NT - 1:
                    pool.wait_ge(kvn_ready, t + 1)
                    if t == 0:
                        nc.gpsimd.tensor_copy(kv_sum[:, 1, :], qkn[:, 0, D:2 * D]).then_inc(sum_ready, 1)
                    else:
                        pool.wait_ge(sum_ready, t)
                        nc.gpsimd.tensor_tensor(kv_sum[:, t + 1, :], kv_sum[:, t, :], qkn[:, t % 2, D:2 * D],
                                                ALU.add).then_inc(sum_ready, 1)
                if t >= 2:
                    k = t - 2
                    pool.wait_ge(u_ready, k + 1)
                    nc.gpsimd.tensor_scalar(h0[:, k % 2, :], x1[:, k % 2, :], mv2[:, k % 2, 0:1], scales[:, k % 2, 0:1],
                                            ALU.subtract, ALU.mult).then_inc(pool_done, 1)
                    pool.wait_ge(pool_done, k + 1)
                    nc.gpsimd.tensor_tensor(base[:, k, :], x1[:, k % 2, :], h0[:, k % 2, :], ALU.add)\
                        .then_inc(base_ready, 1)
            for n in range(2 * NI * NC):
                hf, c, w = PROJECTIONS[n]
                cols = slice(c * BANK, (c + 1) * BANK)
                pool.wait_ge(rest1, n + 1)
                pool.wait_ge(part2, n + 1)
                nc.gpsimd.tensor_tensor(part[w][hf][:, 2, cols], rest[:, n % 2, :], part[w][hf][:, 1, cols],
                                        ALU.subtract).then_inc(part3, 1)
            steps = Counted(pool_steps)
            pool.wait_ge(ld_b, 16)
            pool.wait_ge(pool_steps, steps.mark(nc.gpsimd.tensor_copy(b_parts[:, 0, :], b_sb)))
            pool.wait_ge(pool_steps, steps.mark(
                nc.gpsimd.tensor_tensor(b_rest, b_sb, b_parts[:, 0, :], ALU.subtract)))
            pool.wait_ge(pool_steps, steps.mark(nc.gpsimd.tensor_copy(b_parts[:, 1, :], b_rest)))
            nc.gpsimd.tensor_tensor(b_parts[:, 2, :], b_rest, b_parts[:, 1, :], ALU.subtract).then_inc(bparts_ready, 2)
            pool.wait_ge(ld_mlp, 48)
            for w in (w_in, w_up):
                for i in range(NI):
                    v = steps.mark(nc.gpsimd.tensor_scalar(w[:, i, :], w[:, i, :], lnw[:, 1, i:i + 1], None, ALU.mult))
            pool.wait_ge(pool_steps, v)
            for group, whole, high, low in ((0, w_in, w_in_hi, w_in_lo), (0, w_up, w_up_hi, w_up_lo),
                                            (1, u_t, u_hi, u_lo), (1, w_down, w_down_hi, w_down_lo)):
                pool.wait_ge(pe_pair, 2 * (group + 1) * NSTEP)
                pool.wait_ge(pool_steps, steps.mark(nc.gpsimd.tensor_copy(high[:, :, :], whole[:, :, :])))
                nc.gpsimd.tensor_tensor(low[:, :, :], whole[:, :, :], high[:, :, :].bitcast(F32), ALU.subtract)\
                    .then_inc(wsplit_ready, 1)

        @block.vector
        def _(dve):
            done = Counted(dve_done)

            def need(value):
                dve.wait_ge(dve_done, value)

            dve.wait_ge(ld_x, 16)
            for t in range(NT):
                v = done.mark(nc.vector.bn_stats(stats[:, t, :], x_sb[:, t, :]))
            need(v)
            for t in range(NT):
                v = done.mark(nc.vector.bn_aggr(mv[:, t, :], stats[:, t, :]))
            need(v)
            nc.vector.tensor_scalar(veps[:, :], mv[:, :, 1], LN_EPS, None, ALU.add).then_inc(var_ready, 1)
            dve.wait_ge(std_ready, 1)
            need(done.mark(nc.vector.reciprocal(rstd[:, :], std[:, :])))

            def normalize(t):
                if t >= 2:
                    dve.wait_ge(pe_xt, t - 1)
                nc.vector.tensor_scalar(xn[:, t % 2, :], x_sb[:, t, :], mv[:, t, 0:1], rstd[:, t:t + 1],
                                        ALU.subtract, ALU.mult).then_inc(xn_ready, 1)

            def spread_m():
                dve.wait_ge(m_ready, 1)
                dve.wait_ge(ld_cst, 16)
                for j in range(NI):
                    ins = nc.vector.tensor_tensor(
                        m_block[:, j, :, :], m_sb[:, j, :].unsqueeze(1).broadcast_to([P, HPH, R]),
                        cst[:, C_BLOCK:C_BLOCK + HPH].unsqueeze(2).broadcast_to([P, HPH, R]), ALU.mult)
                ins.then_inc(mblock_ready, 1)

            def energy(t):
                dve.wait_ge(sq_ready, t + 1)
                nc.vector.tensor_reduce(
                    ss[:, t % 2, :], sq[:, t % 2, :].rearrange("p (h s) -> p h s", s=HD), AX.X, ALU.add)\
                    .then_inc(ss_ready, 1)

            def unit(t):
                dve.wait_ge(norm_ready, t + 1)
                need(done.mark(nc.vector.reciprocal(inv_norm[:, t % 2, :], norm[:, t % 2, :])))
                if t >= 2:
                    dve.wait_ge(pe_cum, 2 * (t - 2) + 1)
                    dve.wait_ge(sum_ready, t - 1)
                for half, made in ((1, kvn_ready), (0, qn_ready)):
                    nc.vector.tensor_tensor(
                        qkn[:, t % 2, half * D:(half + 1) * D].rearrange("p (h s) -> p h s", s=HD),
                        PSUM_QK[t % 2][:, half * D:(half + 1) * D].rearrange("p (h s) -> p h s", s=HD),
                        inv_norm[:, t % 2, half * H:(half + 1) * H].unsqueeze(2).broadcast_to([P, H, HD]),
                        ALU.mult).then_inc(made, 1)

            def multiply(t):
                dve.wait_ge(pe_cum, 2 * t + 1)
                dve.wait_ge(qn_ready, t + 1)
                if t >= 2:
                    dve.wait_ge(pe_pt, t - 1)
                q = qkn[:, t % 2, 0:D].rearrange("p (h a s) -> p h a s", a=2, s=HD // 2)
                c = PSUM_C[:, 0:D].rearrange("p (h a s) -> p h a s", a=2, s=HD // 2)
                o = prod[:, t % 2, :].rearrange("p (h a s) -> p h a s", a=2, s=HD // 2)
                v = done.mark(nc.vector.tensor_tensor(prod[:, t % 2, :], qkn[:, t % 2, 0:D], PSUM_C[:, 0:D], ALU.mult))
                for e in range(2):
                    w = done.mark(nc.vector.tensor_tensor(cross[:, t % 2, e, :, :], q[:, :, e, :], c[:, :, 1 - e, :],
                                                          ALU.mult))
                need(v)
                v = done.mark(nc.vector.tensor_tensor(o[:, :, 0, 1:], o[:, :, 0, 1:], o[:, :, 1, 1:], ALU.subtract))
                need(v)
                nc.vector.tensor_tensor(o[:, :, 1, 1:], cross[:, t % 2, 0, :, 1:], cross[:, t % 2, 1, :, 1:],
                                        ALU.add).then_inc(prod_ready, 1)

            def norms(t):
                p = t % 2
                dve.wait_ge(pe_y, t + 1)
                if t >= 2:
                    dve.wait_ge(base_ready, t - 1)
                    dve.wait_ge(pe_ut, t - 1)
                nc.vector.tensor_tensor(x1[:, p, :], x_sb[:, t, :], PSUM_Y[:, 0:D], ALU.add).then_inc(x1_ready, 1)
                dve.wait_ge(x1_ready, t + 1)
                need(done.mark(nc.vector.bn_stats(stats2[:, p, :], x1[:, p, :])))
                need(done.mark(nc.vector.bn_aggr(mv2[:, p, :], stats2[:, p, :])))
                v = done.mark(nc.vector.tensor_scalar(vars2[:, p, 0:1], mv2[:, p, 1:2], LN_EPS, None, ALU.add))
                nc.vector.tensor_scalar(vars2[:, p, 1:2], mv2[:, p, 1:2], 1 + RMS_EPS, LN_EPS * RMS_EPS, ALU.mult,
                                        ALU.add).then_inc(var2_ready, 1)

            def norm_u(t):
                p = t % 2
                dve.wait_ge(std2_ready, t + 1)
                need(done.mark(nc.vector.reciprocal(scales[:, p, :], stds2[:, p, :])))
                nc.vector.tensor_scalar(u[:, p, :], x1[:, p, :], mv2[:, p, 0:1], scales[:, p, 1:2], ALU.subtract, ALU.mult)\
                    .then_inc(u_ready, 1)

            normalize(0)
            for n in range(NT + 4):
                if 0 <= n - 1 < NT:
                    energy(n - 1)
                if 0 <= n - 2 < NT:
                    multiply(n - 2)
                if 0 <= n - 1 < NT:
                    unit(n - 1)
                if 0 <= n - 3 < NT:
                    norms(n - 3)
                if n + 1 < NT:
                    normalize(n + 1)
                if n == 0:
                    spread_m()
                if n == 5:
                    for dst, src in ((ident_b, ident), (later_b, cst[:, C_LATER:C_LATER + P])):
                        nc.vector.tensor_copy(dst[:, :], src).then_inc(masks_ready, 1)
                if 0 <= n - 3 < NT:
                    norm_u(n - 3)

            for n in range(2 * NI * NC):
                hf, c, w = PROJECTIONS[n]
                dve.wait_ge(part1, n + 1)
                if n >= 2:
                    dve.wait_ge(part3, n - 1)
                nc.vector.tensor_tensor(rest[:, n % 2, :], b8[n % 4], part[w][hf][:, 0, c * BANK:(c + 1) * BANK],
                                        ALU.subtract).then_inc(rest1, 1)
                dve.wait_ge(rest1, n + 1)
                nc.vector.tensor_copy(part[w][hf][:, 1, c * BANK:(c + 1) * BANK], rest[:, n % 2, :]).then_inc(part2, 1)

            def maxima(use):
                u, n = USES[use]
                j, i, k, keys = CHUNKS[u % NC][n]
                dve.wait_ge(pe_ring, use + 1)
                if use >= RING:
                    dve.wait_ge(ring_read, use - RING + 1)
                mask = C_MASK + S - (i + 1) * P + k * BANK
                nc.vector.tensor_tensor_reduce(junk[:, use % RING, 0:keys], bank[use % RING][:, 0:keys],
                                               cst[:, mask:mask + keys], 1.0, LOWEST, ALU.add, ALU.max,
                                               mpart[:, u % 2, k, i % QT, j:j + 1]).then_inc(ring_read, 1)

            def split_max(u, use):
                p, full = u % 2, mpart[:, u % 2, 0, :, :]
                dve.wait_ge(ring_read, use + 1)
                if u >= 2:
                    dve.wait_ge(pe_ring, UNIT_READY[u - 2])
                if u % NC:
                    need(done.mark(nc.vector.tensor_tensor(full, full, mpart[:, p, 1, :, :], ALU.max)))
                need(done.mark(nc.vector.tensor_copy(mparts[:, p, :, 0, :], full)))
                need(done.mark(nc.vector.tensor_tensor(mrest[:, :, :], full, mparts[:, p, :, 0, :], ALU.subtract)))
                need(done.mark(nc.vector.tensor_copy(mparts[:, p, :, 1, :], mrest[:, :, :])))
                nc.vector.tensor_tensor(mparts[:, p, :, 2, :], mrest[:, :, :], mparts[:, p, :, 1, :], ALU.subtract)\
                    .then_inc(maxp_ready, 1)

            for use, (of, n) in enumerate(USES):
                if n is None:
                    dve.wait_ge(pe_ring, use + 1)
                    if of >= 2:
                        dve.wait_ge(max_landed[of - 2], 16)
                    nc.vector.tensor_copy(mrows[:, of % 2, :], bank[use % RING][0:MROWS * G, :])\
                        .then_inc(ring_read, 1)
                else:
                    maxima(use)
                    if n == len(CHUNKS[of % NC]) - 1:
                        split_max(of, use)

            def by_token(t):
                o = bank[t % 2][:, :].rearrange("p (h v) -> p h v", v=VW)
                dve.wait_ge(pe_ot, t + 1)
                need(done.mark(nc.vector.reciprocal(linv[:, t % 2, :], o[:, :, R])))
                nc.vector.tensor_tensor(onorm[:, t % 2, :, :], o[:, :, 0:R],
                                        linv[:, t % 2, :].unsqueeze(2).broadcast_to([P, H, R]), ALU.mult)\
                    .then_inc(lsum_read, 1)
                dve.wait_ge(lsum_read, t + 1)
                nc.vector.tensor_reduce(attn_a[:, t, :], onorm[:, t % 2, :, :].rearrange("p h r -> p r h"),
                                        AX.X, ALU.add).then_inc(attn_ready, 1)

            def modulate(c):
                toks = slice(c * QT, (c + 1) * QT)
                m, rest_m, parts = mod_h[:, toks, :], mod_rest[:, toks, :], mod_parts[:, toks, :, :]

                def spread_part(src, first, slots):
                    return done.mark(nc.vector.tensor_copy(parts[:, :, first:first + slots, :],
                                                           src.unsqueeze(2).broadcast_to([P, QT, slots, R])))

                dve.wait_ge(tanh_ready, c + 1)
                need(done.mark(nc.vector.scalar_tensor_tensor(m, tanh_a[:, toks, :], MOD_SCALE, ha[:, toks, :],
                                                              ALU.mult, ALU.mult)))
                need(spread_part(m, 0, 3))
                need(done.mark(nc.vector.tensor_tensor(rest_m, m, parts[:, :, 0, :], ALU.subtract)))
                need(spread_part(rest_m, 3, 2))
                nc.vector.tensor_tensor(parts[:, :, 5, :], rest_m, parts[:, :, 3, :], ALU.subtract)\
                    .then_inc(mparts_ready, 1)

            dve.wait_ge(vals_ready, 2 * NT)
            for c in range(NC):
                for t in range(c * QT, (c + 1) * QT):
                    by_token(t)
                modulate(c)

            def low(n):
                c, f = divmod(n, NF)
                toks = slice(c * BANK, (c + 1) * BANK)
                dve.wait_ge(high_ready, n + 1)
                nc.vector.tensor_tensor(hidden[f][:, 1, toks], gate[:, n % 4, :], hidden[f][:, 0, toks].bitcast(F32),
                                        ALU.subtract).then_inc(hid_ready, 1)

            for n in range(NF * NC):
                dve.wait_ge(silu_ready, n + 1)
                dve.wait_ge(pe_up, n + 1)
                nc.vector.tensor_tensor(gate[:, n % 4, :], gate[:, n % 4, :], b8[2 + n % 2], ALU.mult).then_inc(gated, 1)
                if n >= 1:
                    low(n - 1)
            low(NF * NC - 1)
            dve.wait_ge(base_ready, NT)
            for t in range(NT):
                dve.wait_ge(pe_down, t + 1)
                nc.vector.tensor_tensor(y_sb[:, t, :], b8[4 + t % 4][:, 0:D], base[:, t, :], ALU.add).then_inc(y_ready, 1)


def by_row_of_head(w):
    return np.asarray(w).reshape(NG, G, HD, D).transpose(3, 0, 2, 1).reshape(D, D)


def kernel(L0_attn_x, L0_attn_W_q, L0_attn_W_kv, L0_attn_W_o, L0_ffn_ln1_w, L0_ffn_ln2_w, L0_ffn_Wq, L0_ffn_Wk,
           L0_ffn_Wv, L0_ffn_Wo, L0_ffn_A, L0_ffn_B, L0_ffn_W_in_base, L0_ffn_W_up_base, L0_ffn_W_down):
    from concourse import bacc
    from concourse.bass_utils import run_bass_kernel_spmd

    nc = bacc.Bacc("TRN2", target_bir_lowering=False, num_devices=1)
    arrays = {
        "x": np.asarray(L0_attn_x).reshape(S, D),
        "wq": L0_attn_W_q,
        "wkv": L0_attn_W_kv,
        "wo_t": np.asarray(L0_attn_W_o).T,
        "ln": np.stack([np.asarray(w).reshape(NI, P) for w in (L0_ffn_ln1_w, L0_ffn_ln2_w)]).transpose(2, 0, 1),
        "fwq_t": by_row_of_head(L0_ffn_Wq),
        "fwk_t": by_row_of_head(L0_ffn_Wk),
        "fwv": L0_ffn_Wv,
        "fwo": L0_ffn_Wo,
        "a": L0_ffn_A,
        "b": L0_ffn_B,
        "win_t": np.asarray(L0_ffn_W_in_base).T,
        "wup_t": np.asarray(L0_ffn_W_up_base).T,
        "wdown_t": np.asarray(L0_ffn_W_down).T,
        "consts": constants(),
    }
    arrays = {f"in_{k}": np.ascontiguousarray(v) for k, v in arrays.items()}
    args = [nc.dram_tensor(k, v.shape, mybir.dt.from_np(v.dtype), kind="ExternalInput").ap() for k, v in arrays.items()]
    out = nc.dram_tensor("out", (S, D), F32, kind="ExternalOutput").ap()
    seq_preln_kernel(nc, *args, out)
    r = run_bass_kernel_spmd(nc, [arrays], core_ids=[0])
    return r.results[0]["out"].reshape(1, S, D)
```

```python
from contextlib import ExitStack

import concourse.bass as bass
import numpy as np
from concourse import mybir

P = 128
S = 1024
D = 256
H = 16
HD = D // H
F = 1024
R = 16
NT = S // P
NI = D // P
NF = F // P
BANK = 512
NC = S // BANK
HPH = P // HD
G = 4
NG = H // G
VW = 32
SLOTS = 6
KROWS = SLOTS * HD
MROWS = 3
LN_EPS = 1e-5
RMS_EPS = 1e-6
MOD_SCALE = 0.1
LOWEST = float(np.finfo(np.float32).min)
ALIGNED = 32
MASKED = -2.0 ** 127

ALU = mybir.AluOpType
ACT = mybir.ActivationFunctionType
AX = mybir.AxisListType
F32 = mybir.dt.float32
BF16 = mybir.dt.bfloat16
F32R = mybir.dt.float32r

Q_PART = (0, 0, 0, 1, 1, 2)
K_PART = (0, 1, 2, 0, 1, 0)

C_DFT, C_IDFT, C_IDENT, C_TRI, C_ONES, C_LATER, C_BLOCK, C_MASK, C_END = (
    0, 128, 256, 384, 512, 640, 768, 776, 776 + S)


def constants():
    n, k = np.arange(HD)[:, None], np.arange(1, HD // 2)[None, :]
    angle = 2 * np.pi * n * k / HD
    dft = np.zeros((HD, HD))
    dft[:, 0] = 1 / np.sqrt(HD)
    dft[:, 1:HD // 2] = np.cos(angle) * np.sqrt(2 / HD)
    dft[:, HD // 2] = (-1.0) ** n[:, 0] / np.sqrt(HD)
    dft[:, HD // 2 + 1:] = -np.sin(angle) * np.sqrt(2 / HD)
    inv = np.zeros((HD, HD))
    inv[0] = 1 / HD
    inv[1:HD // 2] = np.cos(angle).T / HD
    inv[HD // 2] = (-1.0) ** n[:, 0] / HD
    inv[HD // 2 + 1:] = -np.sin(angle).T / HD
    c = np.zeros((P, C_END), np.float32)
    c[:, C_DFT:C_DFT + P] = np.kron(np.eye(HPH), dft)
    c[:, C_IDFT:C_IDFT + P] = np.kron(np.eye(HPH), inv.T)
    c[:, C_IDENT:C_IDENT + P] = np.eye(P)
    c[:, C_TRI:C_TRI + P] = np.triu(np.ones((P, P)))
    c[:, C_ONES:C_ONES + P] = 1
    c[:, C_LATER:C_LATER + P] = np.tril(np.ones((P, P)), -1) * MASKED
    c[:, C_BLOCK:C_BLOCK + HPH] = np.kron(np.eye(HPH), np.ones((HD, 1)))
    c[:, C_MASK + S - P:C_MASK + S] = np.where(np.triu(np.ones((P, P)), 1) > 0, LOWEST, 0)
    return c


def attention_steps():
    return [(c, b, max(0, b * P - c * BANK)) for c in range(NC) for b in range((c + 1) * BANK // P)]


def score_chunks(c):
    tiles = BANK // P
    return [(j, i, k, min(BANK, (i + 1) * P - k * BANK))
            for j in range(G) for i in range(c * tiles, (c + 1) * tiles) for k in range(c + 1)]


STEPS = attention_steps()
NSTEP = len(STEPS)
CHUNKS = [score_chunks(c) for c in range(NC)]
NU = NG * NC
QT = BANK // P
RING = 3
PRING = 6
TURN_AFTER = 2


def ring_uses():
    uses = []
    for u in range(NU):
        for n in range(len(CHUNKS[u % NC])):
            uses.append((u, n))
            if u >= 1 and n == TURN_AFTER - 1:
                uses.append((u - 1, None))
    return uses + [(NU - 1, None)]


USES = ring_uses()
UNIT_READY = [USES.index((u, None)) + 1 for u in range(NU)]
RING_USE, PAIR, WEIGH, PROJECT, VALUES = "ring use", "pair", "weigh", "project", "values"


FIRST_STACKS, NEXT_STACKS = 8500, 15500


def attention_order():
    handoff, dma = 100, 2500
    stacks = {0: FIRST_STACKS, 1: NEXT_STACKS}
    pe = act = 0.0
    dve = 1500.0
    order = []
    ring_free, landed, exp_done, weighed = {}, {}, {}, {}
    split_done, pv_free = {}, 0.0
    use = m = step = tile = 0
    project = 2 * NC
    never = float("inf")
    while step < NG * NSTEP:
        at_use = at_pair = at_weigh = at_project = at_values = never
        if use < len(USES):
            u, n = USES[use]
            at_use = max(ring_free.get(use - RING, 0), split_done[u] if n is None else stacks.get(u, 0))
        if project < 2 * NC * NI:
            at_project = 0
        elif tile < NT:
            at_values = parts_done if tile == 1 else 0
        elif m < 2 * NG * NSTEP:
            g, n = divmod(m // 2, NSTEP)
            if m < PRING or (m - PRING) // 2 in weighed:
                at_pair = max(landed.get(g * NC + STEPS[n][0], never), exp_done.get(m - 2, 0))
        if 2 * step + 1 in exp_done:
            at_weigh = max(exp_done[2 * step + 1], pv_free if STEPS[step % NSTEP][1] == 0 else 0)
        start, _, kind = min((max(pe, at), rank, kind) for rank, (at, kind) in enumerate((
            (at_use, RING_USE), (at_pair, PAIR), (at_weigh, WEIGH), (at_project, PROJECT), (at_values, VALUES))))
        if kind == RING_USE:
            order.append((kind, use))
            if USES[use][1] is None:
                pe = start + 220
                dve = max(dve, pe + handoff) + 600
                landed[USES[use][0]] = dve + dma
            else:
                u, n = USES[use]
                keys = CHUNKS[u % NC][n][3]
                pe = start + keys * 0.42
                dve = max(dve, pe + handoff) + 70 + keys * 1.04
                if n == len(CHUNKS[u % NC]) - 1:
                    dve += 500
                    split_done[u] = dve + handoff
            ring_free[use] = dve + handoff
            use += 1
        elif kind == PROJECT:
            order.append((kind, project))
            pe = start + 1720
            act = max(act, pe + handoff) + 500
            parts_done = dve = max(dve, act + handoff) + 950
            project += 1
        elif kind == VALUES:
            order.append((kind, tile))
            pe = start + 910
            act = max(act, pe + handoff) + 350
            tile += 1
        elif kind == PAIR:
            order.append((kind, m))
            c, b, q0 = STEPS[m // 2 % NSTEP]
            pe = start + 2 * (BANK - q0) * 0.42 + (110 if b * P >= c * BANK else 0)
            buffer_free = weighed[(m - PRING) // 2] if m >= PRING else 0
            act = max(act, pe + handoff, buffer_free) + 50 + 2 * (BANK - q0) * 0.84
            exp_done[m] = act + handoff
            m += 1
        else:
            order.append((kind, step))
            c, b, q0 = STEPS[step % NSTEP]
            pe = start + (BANK - q0) * 1.83
            weighed[step] = pe
            if b == (c + 1) * BANK // P - 1:
                act = max(act, pe + handoff) + 480
                pv_free = act + handoff
            step += 1
    return order


ORDER = attention_order()


PROJECTIONS = [(hf, c, w) for hf in range(NI) for c in range(NC) for w in range(2)]
FIRST_TURN = NG * NSTEP - 7
EARLY = 2

SLOT_RUNS = (((0, 3, 0), (3, 2, 1), (5, 1, 2)), ((0, 3, 0), (3, 2, 0), (5, 1, 0)))
STACK_LOADS = sum(map(len, SLOT_RUNS))


class Counted:

    def __init__(self, sem):
        self.sem, self.value = sem, 0

    def mark(self, ins, by=1):
        ins.then_inc(self.sem, by)
        self.value += by
        return self.value


def seq_preln_kernel(nc, x, wq, wkv, wo_t, ln, fwq_t, fwk_t, fwv, fwo, a, b, win_t, wup_t,
                     wdown_t, consts, out):
    with ExitStack() as ctx:
        def sb(name, shape, dt=F32):
            return ctx.enter_context(nc.sbuf_tensor(name, shape, dt))

        def sem(name):
            return ctx.enter_context(nc.semaphore(name))

        def next_base():
            return -(-nc.sbuf_base // ALIGNED) * ALIGNED

        class Region:

            def __init__(self, name, columns):
                self.base = next_base()
                self.all, self.at = sb(name, [P, columns]), 0

            def take(self, *shape, dt=F32):
                n = int(np.prod(shape)) * (1 if dt == F32 else 0.5)
                assert n == int(n) and self.at + n <= self.all.shape[1]
                v = self.all[:, self.at:self.at + int(n)]
                self.at += int(n)
                if dt != F32:
                    v = v.bitcast(dt)
                axes = " ".join(f"a{k}" for k in range(len(shape)))
                sizes = {f"a{k}": shape[k] for k in range(1, len(shape))}
                return v.rearrange(f"p ({axes}) -> p {axes}", **sizes) if len(shape) > 1 else v

            def again(self):
                self.at = 0
                return self

        def placed(name, shape, base, offset=0):
            return nc.alloc_sbuf_tensor_at(name, shape, F32R, offset=base + offset)

        spread = nc.dram_tensor("spread", (2, 3, NC, NG, HD, G * BANK), BF16, kind="Internal").ap()

        region_a = Region("region_a", 6144)
        region_b = Region("region_b", 4096)
        region_c = Region("region_c", 6144)
        region_d = Region("region_d", 4096)
        region_e = Region("region_e", 1024)
        cst = sb("cst", [P, C_END])
        dft, idft = cst[:, C_DFT:C_DFT + P], cst[:, C_IDFT:C_IDFT + P]
        ident, tri = cst[:, C_IDENT:C_IDENT + P], cst[:, C_TRI:C_TRI + P]
        ones = cst[:, C_ONES:C_ONES + P]
        x_sb = region_b.take(NT, D)
        w_q = region_a.take(NI, D)
        w_kv = region_a.take(NI, D)
        w_o = region_a.take(NI, D)
        f_q = region_e.take(NI, D)
        f_k = region_e.take(NI, D)
        f_v = region_a.take(NI, D)
        f_o = region_a.take(NI, D)
        a_sb = sb("a_sb", [P, NI, R])
        lnw = sb("lnw", [P, 2, NI])
        spec_w = region_a.take(NI, 2 * D)
        spec_o = region_a.take(NI, D)
        m_sb = sb("m_sb", [P, NI, R])
        m_block = sb("m_block", [P, NI, HPH, R])
        w_u = sb("w_u", [P, NI, D + R])
        stats = sb("stats", [P, NT, 6])
        mv = sb("mv", [P, NT, 2])
        veps = sb("veps", [P, NT])
        std = sb("std", [P, NT])
        rstd = sb("rstd", [P, NT])
        bias = sb("bias", [P, NT])
        xn = region_d.take(2, D)
        xn_t = region_d.take(2, D)
        sq = region_a.take(2, 2 * D)
        ss = sb("ss", [P, 2, 2 * H])
        norm = sb("norm", [P, 2, 2 * H])
        inv_norm = sb("inv_norm", [P, 2, 2 * H])
        qkn = region_a.take(2, 2 * D)
        kv_sum = region_b.take(NT, D)
        prod = region_d.take(2, D)
        cross = region_d.take(2, 2, H, HD // 2)
        prod_t = region_d.take(2, D)
        x1 = region_d.take(2, D)
        stats2 = sb("stats2", [P, 2, 6])
        mv2 = sb("mv2", [P, 2, 2])
        vars2 = sb("vars2", [P, 2, 2])
        stds2 = sb("stds2", [P, 2, 2])
        scales = sb("scales", [P, 2, 2])
        u = region_d.take(2, D)
        h0 = region_d.take(2, D)
        base = sb("base", [P, NT, D])
        ut_base, u_t = next_base(), sb("u_t", [P, NI, S])
        part = [[region_c.take(3, S, dt=BF16) for hf in range(NI)] for w in range(2)]
        rest = sb("rest", [P, 2, BANK])
        q_base, q_stack = next_base(), sb("q_stack", [P, NG, NC, G, BANK], BF16)
        k_base, k_stack = next_base(), sb("k_stack", [P, NG, NC, G, BANK], BF16)
        vals_base, vals = next_base(), sb("vals", [P, NT, H, VW])
        ha = sb("ha", [P, NT, R])
        probs = region_a.again().take(PRING, 2, BANK)
        ident_b, later_b = sb("ident_b", [P, P], BF16), sb("later_b", [P, P], BF16)
        junk = sb("junk", [P, RING, BANK], BF16)
        mpart = sb("mpart", [P, 2, NC, QT, G])
        mrest = sb("mrest", [P, QT, G])
        mparts = sb("mparts", [P, 2, QT, MROWS, G], BF16)
        mrows = sb("mrows", [MROWS * G, 2, BANK], BF16)
        o_t = region_b.again().take(NG, S)
        linv = sb("linv", [P, 2, H])
        onorm = sb("onorm", [P, 2, H, R])
        attn_a = sb("attn_a", [P, NT, R])
        tanh_a = sb("tanh_a", [P, NT, R])
        mod_h = sb("mod_h", [P, NT, R])
        region_e.again()
        mod_rest = onorm[:, 0, 0:NT, :]
        mod_parts = region_e.take(NT, SLOTS, R, dt=BF16)
        mod_t = region_e.take(S, dt=BF16)[0:KROWS, :]
        region_d.again()
        b_sb, b_rest = region_d.take(F)[0:R, :], region_d.take(F)[0:R, :]
        b_parts = region_d.take(3, F, dt=BF16)[0:R, :, :]
        b_stack = region_d.take(F, dt=BF16)[0:KROWS, :]

        region_c.again()
        w_in, w_up, w_down = region_c.take(NI, F), region_c.take(NI, F), region_c.take(NF, D)
        W = 4 * NI * F
        w_in_lo = placed("w_in_lo", [P, NI, F], region_c.base)
        w_up_lo = placed("w_up_lo", [P, NI, F], region_c.base, W)
        w_down_lo = placed("w_down_lo", [P, NF, D], region_c.base, 2 * W)
        u_lo = placed("u_lo", [P, NI, S], ut_base)
        group_bytes = 2 * G * S
        w_in_hi = placed("w_in_hi", [P, NI, F], q_base)
        w_up_hi = placed("w_up_hi", [P, NI, F], k_base)
        u_hi = placed("u_hi", [P, NI, S], q_base, group_bytes)
        w_down_hi = placed("w_down_hi", [P, NF, D], k_base, group_bytes)
        H_BYTES = 4 * 2 * S
        places = [(region_a.base, 0), (region_a.base, H_BYTES), (region_a.base, 2 * H_BYTES),
                  (q_base, 2 * group_bytes), (q_base, 3 * group_bytes),
                  (k_base, 2 * group_bytes), (k_base, 3 * group_bytes), (vals_base, 0)]
        hidden = [placed(f"hidden{f}", [P, 2, S], *places[f]) for f in range(NF)]
        gate = vals[:, NT // 2:, :, :].rearrange("p t h v -> p (t h v)").rearrange("p (n m) -> p n m", m=BANK)
        y_sb = region_b.again().take(NT, D)

        bank = [ctx.enter_context(nc.psum_tensor(f"bank{n}", [P, BANK], F32)) for n in range(4, 7)]
        pair = [ctx.enter_context(nc.psum_tensor(f"pair{n}", [P, 2, BANK], F32)) for n in range(2)]
        pv = ctx.enter_context(nc.psum_tensor("pv", [P, BANK], F32))
        b8 = [pair[0][:, 0, :], pair[0][:, 1, :], pair[1][:, 0, :], pair[1][:, 1, :],
              bank[0][:, :], bank[1][:, :], bank[2][:, :], pv[:, :]]

        ld_x = [sem(f"ld_x{n}") for n in range(NC)]
        ld_wo, ld_mask, ld_cst, ld_spec, ld_attn, ld_ln, ld_mlp, ld_b, b_stacked = (
            sem(f"ld_{n}") for n in ("wo", "mask", "cst", "spec", "attn", "ln", "mlp", "b", "b_stacked"))
        parts_out = [sem(f"parts_out{n}") for n in range(NI)]
        first_stacked, stacked = sem("first_stacked"), [sem(f"stacked{n}") for n in range(NG)]
        max_landed = [sem(f"max_landed{n}") for n in range(NU)]
        stored = sem("stored")
        pe_spec, pe_speco, pe_m, pe_wu = sem("pe_spec"), sem("pe_speco"), sem("pe_m"), sem("pe_wu")
        pe_xt, pe_qk, pe_cum, pe_pt, pe_y, pe_ut = (sem(f"pe_{n}") for n in ("xt", "qk", "cum", "pt", "y", "ut"))
        pe_proj, pe_vals = sem("pe_proj"), sem("pe_vals")
        pe_ring, pe_pair, pe_pv = sem("pe_ring"), sem("pe_pair"), sem("pe_pv")
        pe_ot, pe_modt, pe_gate, pe_up, pe_down = (sem(f"pe_{n}") for n in ("ot", "modt", "gate", "up", "down"))
        spec_ready, speco_ready, m_ready, mblock_ready, wu_ready = (
            sem(n) for n in ("spec_ready", "speco_ready", "m_ready", "mblock_ready", "wu_ready"))
        xn_ready, xt_ready, sq_ready, kvn_ready, qn_ready, sum_ready = (
            sem(n) for n in ("xn_ready", "xt_ready", "sq_ready", "kvn_ready", "qn_ready", "sum_ready"))
        prod_ready, pt_ready, x1_ready, u_ready, base_ready, ut_ready = (
            sem(n) for n in ("prod_ready", "pt_ready", "x1_ready", "u_ready", "base_ready", "ut_ready"))
        bias_ready = sem("bias_ready")
        scaled_attn, pool_set = sem("scaled_attn"), sem("pool_set")
        part1, rest1, part2, part3 = (sem(n) for n in ("part1", "rest1", "part2", "part3"))
        vals_ready = sem("vals_ready")
        var_ready, std_ready, ss_ready, norm_ready, var2_ready, std2_ready = (
            sem(n) for n in ("var_ready", "std_ready", "ss_ready", "norm_ready", "var2_ready", "std2_ready"))
        ring_read, exp_ready, masks_ready, maxp_ready, ot_ready = (
            sem(n) for n in ("ring_read", "exp_ready", "masks_ready", "maxp_ready", "ot_ready"))
        lsum_read, attn_ready, tanh_ready, modt_ready = (
            sem(n) for n in ("lsum_read", "attn_ready", "tanh_ready", "modt_ready"))
        bparts_ready, wsplit_ready, mparts_ready = sem("bparts_ready"), sem("wsplit_ready"), sem("mparts_ready")
        silu_ready, gated, high_ready, hid_ready, y_ready = (
            sem(n) for n in ("silu_ready", "gated", "high_ready", "hid_ready", "y_ready"))
        dve_done = sem("dve_done")
        pool_done, pool_steps = sem("pool_done"), sem("pool_steps")
        block = ctx.enter_context(nc.Block())

        VALUE_BANKS, UP_BANKS = (b8[7], b8[0], b8[1]), (b8[2], b8[3], b8[7])
        PSUM_T, PSUM_QK, PSUM_C, PSUM_PT, PSUM_Y, PSUM_UT = b8[0], (b8[1], b8[2]), b8[3], b8[4], b8[5], b8[6]

        @block.sync
        def _(sp):
            def rows(w):
                return w.rearrange("(n p) m -> p n m", p=P)

            sp.dma_start(cst[:, 0:C_MASK], consts[:, 0:C_MASK]).then_inc(ld_cst, 16)
            for dst, src in ((w_q, wq), (w_kv, wkv)):
                sp.dma_start(dst[:, :, :], rows(src)).then_inc(ld_spec, 16)
            for c in range(NC):
                sp.dma_start(x_sb[:, c * QT:(c + 1) * QT, :], rows(x)[:, c * QT:(c + 1) * QT, :]).then_inc(ld_x[c], 16)
                if c == 0:
                    sp.dma_start(w_o[:, :, :], rows(wo_t)).then_inc(ld_wo, 16)
            sp.dma_start(lnw[:, :, :], ln).then_inc(ld_ln, 16)
            for dst, src in ((f_q, fwq_t), (f_k, fwk_t), (f_v, fwv), (f_o, fwo), (a_sb, a)):
                sp.dma_start(dst[:, :, :], rows(src)).then_inc(ld_attn, 16)
            sp.dma_start(cst[:, C_MASK:], consts[:, C_MASK:]).then_inc(ld_mask, 16)

            def load_stacks(g, c, landed):
                for w, stack in enumerate((q_stack, k_stack)):
                    for slot, slots, part0 in SLOT_RUNS[w]:
                        src = spread[w, part0:part0 + (slots if w else 1), c, g]
                        sp.dma_start(stack[slot * HD:(slot + slots) * HD, g, c, :, :],
                                     src.broadcast_to([slots, HD, G * BANK])).then_inc(landed, 16)

            for n, (hf, c, w) in enumerate(PROJECTIONS):
                sp.wait_ge(part1, n + 1)
                sp.wait_ge(part2, n + 1)
                sp.wait_ge(part3, n + 1)
                sp.dma_start(
                    spread.rearrange("w k c g d (h n) -> w c (g d h) k n", h=G)[w, c, hf * P:(hf + 1) * P, :, :],
                    part[w][hf][:, :, c * BANK:(c + 1) * BANK]).then_inc(parts_out[hf], 16)
                if n == 1:
                    sp.wait_ge(parts_out[0], 16 * 2)
                    load_stacks(0, 0, first_stacked)
                if n == 2 * NC - 1:
                    sp.wait_ge(parts_out[0], 16 * 2 * NC)
                    load_stacks(0, 1, stacked[0])
            for un in range(NU):
                g, c = divmod(un, NC)
                sp.wait_ge(ring_read, UNIT_READY[un])
                sp.dma_start(q_stack[KROWS:KROWS + MROWS, g, c, :, :],
                             mrows[:, un % 2, :]).then_inc(max_landed[un], 16)
                if un < NG - 1:
                    sp.wait_ge(parts_out[(un + 1) * NI // NG], 16 * 2 * NC)
                    for half in range(NC):
                        load_stacks(un + 1, half, stacked[un + 1])
                if un == 1:
                    sp.wait_ge(base_ready, NT)
                    sp.wait_ge(pe_ut, NT)
                    sp.dma_start(b_sb, b).then_inc(ld_b, 16)
                    for dst, src in ((w_in, win_t), (w_up, wup_t), (w_down, wdown_t)):
                        sp.dma_start(dst[:, :, :], rows(src)).then_inc(ld_mlp, 16)
                if un == 4:
                    sp.wait_ge(bparts_ready, 2)
                    for slot in range(SLOTS):
                        sp.dma_start(b_stack[slot * R:(slot + 1) * R, :], b_parts[:, K_PART[slot], :])\
                            .then_inc(b_stacked, 16)
            for t in range(NT):
                sp.wait_ge(y_ready, t + 1)
                sp.dma_start(out[t * P:(t + 1) * P, :], y_sb[:, t, :]).then_inc(stored, 16)
            sp.wait_ge(stored, 16 * NT)

        @block.tensor
        def _(pe):
            def spectral_weights():
                pe.wait_ge(ld_cst, 16)
                pe.wait_ge(ld_spec, 32)
                for i in range(NI):
                    for w, src in enumerate((w_q, w_kv)):
                        for o in range(NI):
                            last = nc.tensor.matmul(b8[4 + i][:, w * D + o * P:w * D + (o + 1) * P],
                                                    src[:, o, i * P:(i + 1) * P], dft, start=True, stop=True)
                    last.then_inc(pe_spec, 1)

            def spectral_output():
                pe.wait_ge(ld_wo, 16)
                for o in range(NI):
                    last = nc.tensor.matmul(b8[6][:, o * D:(o + 1) * D], idft, w_o[:, o, :], start=True, stop=True)
                last.then_inc(pe_speco, 1)

            def m_weights():
                pe.wait_ge(ld_attn, 80)
                for j in range(NI):
                    for o in range(NI):
                        last = nc.tensor.matmul(b8[7][:, j * R:(j + 1) * R], f_o[:, o, j * P:(j + 1) * P], a_sb[:, o, :],
                                                start=(o == 0), stop=(o == NI - 1))
                last.then_inc(pe_m, 1)

            def value_weights():
                pe.wait_ge(mblock_ready, 1)
                for i in range(NI):
                    for j in range(NI):
                        last = nc.tensor.matmul(b8[7][:, i * D + j * P:i * D + (j + 1) * P],
                                                f_v[:, j, i * P:(i + 1) * P], m_block[:, j, :, :],
                                                start=True, stop=True)
                last.then_inc(pe_wu, 1)

            def turn_x(t):
                pe.wait_ge(xn_ready, t + 1)
                if t >= 1:
                    pe.wait_ge(xt_ready, t)
                for i in range(NI):
                    last = nc.tensor.transpose(PSUM_T[:, i * P:(i + 1) * P], xn[:, t % 2, i * P:(i + 1) * P], ident)
                last.then_inc(pe_xt, 1)

            def project_qk(t):
                if t == 0:
                    pe.wait_ge(spec_ready, NI)
                pe.wait_ge(xt_ready, t + 1)
                if t >= 2:
                    pe.wait_ge(qn_ready, t - 1)
                for i in range(NI):
                    last = nc.tensor.matmul(PSUM_QK[t % 2], xn_t[:, t % 2, i * P:(i + 1) * P], spec_w[:, i, :],
                                            start=(i == 0), stop=(i == NI - 1))
                last.then_inc(pe_qk, 1)

            def cumulate(t):
                pe.wait_ge(kvn_ready, t + 1)
                if t >= 1:
                    pe.wait_ge(prod_ready, t)
                nc.tensor.matmul(PSUM_C[:, 0:D], tri, qkn[:, t % 2, D:2 * D], start=True,
                                 stop=(t == 0)).then_inc(pe_cum, 1)
                if t >= 1:
                    pe.wait_ge(sum_ready, t)
                    nc.tensor.matmul(PSUM_C[:, 0:D], ones, kv_sum[:, t, :], start=False, stop=True).then_inc(pe_cum, 1)

            def turn_prod(t):
                pe.wait_ge(prod_ready, t + 1)
                if t == 0:
                    pe.wait_ge(spec_ready, NI)
                if t >= 1:
                    pe.wait_ge(pt_ready, t)
                for i in range(NI):
                    last = nc.tensor.transpose(PSUM_PT[:, i * P:(i + 1) * P], prod[:, t % 2, i * P:(i + 1) * P], ident)
                last.then_inc(pe_pt, 1)

            def project_o(t):
                pe.wait_ge(pt_ready, t + 1)
                if t == 0:
                    pe.wait_ge(speco_ready, 1)
                if t >= 1:
                    pe.wait_ge(x1_ready, t)
                for i in range(NI):
                    last = nc.tensor.matmul(PSUM_Y[:, 0:D], prod_t[:, t % 2, i * P:(i + 1) * P], spec_o[:, i, :],
                                            start=(i == 0), stop=(i == NI - 1))
                last.then_inc(pe_y, 1)

            def turn_u(t):
                pe.wait_ge(u_ready, t + 1)
                if t >= 1:
                    pe.wait_ge(ut_ready, t)
                for i in range(NI):
                    last = nc.tensor.transpose(PSUM_UT[:, i * P:(i + 1) * P], u[:, t % 2, i * P:(i + 1) * P], ident)
                last.then_inc(pe_ut, 1)

            def project_part(n):
                hf, c, w = PROJECTIONS[n]
                weights = (f_q, f_k)[w]
                if n == 0:
                    pe.wait_ge(scaled_attn, 2 * NI)
                    pe.wait_ge(xt_ready, NT)
                elif n < 3:
                    pe.wait_ge(qn_ready, NT - 2 + n)
                elif n == 3:
                    pe.wait_ge(prod_ready, NT)
                else:
                    pe.wait_ge(rest1, n - 3)
                pe.wait_ge(ut_ready, (c + 1) * BANK // P)
                for i in range(NI):
                    last = nc.tensor.matmul(b8[n % 4], weights[:, i, hf * P:(hf + 1) * P],
                                            u_t[:, i, c * BANK:(c + 1) * BANK],
                                            start=(i == 0), stop=(i == NI - 1))
                last.then_inc(pe_proj, 1)

            spectral_weights()
            spectral_output()
            turn_x(0)
            for n in range(NT + 4):
                if n + 1 < NT:
                    turn_x(n + 1)
                if 0 <= n - 3 < NT:
                    project_o(n - 3)
                if n < NT:
                    project_qk(n)
                if 0 <= n - 4 < NT:
                    turn_u(n - 4)
                if n == 0:
                    m_weights()
                if n == 2:
                    value_weights()
                if n == NT:
                    project_part(0)
                if 0 <= n - 2 < NT:
                    turn_prod(n - 2)
                if 0 <= n - 1 < NT:
                    cumulate(n - 1)
                if n == NT + 2:
                    project_part(1)

            for n in range(EARLY, 2 * NC):
                project_part(n)
            def values(t):
                if t == 0:
                    pe.wait_ge(wu_ready, 2 * NI)
                if t == 1:
                    pe.wait_ge(rest1, 2 * NI * NC)
                if t >= 3:
                    pe.wait_ge(vals_ready, 2 * (t - 2))
                for i in range(NI):
                    last = nc.tensor.matmul(VALUE_BANKS[t % 3][:, 0:D + R], u_t[:, i, t * P:(t + 1) * P], w_u[:, i, :],
                                            start=(i == 0), stop=(i == NI - 1))
                last.then_inc(pe_vals, 1)

            def use_ring(use):
                u, n = USES[use]
                if use >= RING:
                    pe.wait_ge(ring_read, use - RING + 1)
                if n is None:
                    pe.wait_ge(maxp_ready, u + 1)
                    for i in range(QT):
                        last = nc.tensor.matmul(bank[use % RING][0:MROWS * G, i * P:(i + 1) * P],
                                                mparts[:, u % 2, i, :, :], ident_b[:, :], start=True, stop=True)
                    last.then_inc(pe_ring, 1)
                    return
                j, i, k, keys = CHUNKS[u % NC][n]
                g = u // NC
                if u == 0 and n == 0:
                    pe.wait_ge(first_stacked, 16 * STACK_LOADS)
                elif u == 1 and n == 0:
                    pe.wait_ge(stacked[0], 16 * STACK_LOADS)
                elif u % NC == 0 and n == 0:
                    pe.wait_ge(stacked[g], 16 * STACK_LOADS * NC)
                nc.tensor.matmul(bank[use % RING][:, 0:keys],
                                 q_stack[0:KROWS, g, i // QT, j, i % QT * P:(i % QT + 1) * P],
                                 k_stack[0:KROWS, g, k, j, 0:keys],
                                 start=True, stop=True).then_inc(pe_ring, 1)

            def score_pair(m):
                (g, n), d = divmod(m // 2, NSTEP), m % 2
                c, b, q0 = STEPS[n]
                if d == 0 and b == 0:
                    pe.wait_ge(max_landed[g * NC + c], 16)
                if m >= 2:
                    pe.wait_ge(exp_ready, m - 1)
                for e in range(2):
                    j = 2 * d + e
                    last = nc.tensor.matmul(pair[m % 2][:, e, 0:BANK - q0],
                                            k_stack[0:KROWS + MROWS, g, b // QT, j, b % QT * P:(b % QT + 1) * P],
                                            q_stack[0:KROWS + MROWS, g, c, j, q0:BANK],
                                            start=True, stop=(b * P < c * BANK))
                    if b * P >= c * BANK:
                        last = nc.tensor.matmul(pair[m % 2][:, e, 0:P], ident_b[:, :], later_b[:, :],
                                                start=False, stop=True)
                last.then_inc(pe_pair, 1)

            def weigh(g, n):
                c, b, q0 = STEPS[n]
                m = (g * NSTEP + n) * 2
                pe.wait_ge(exp_ready, m + 2)
                if b == 0 and g * NC + c >= 1:
                    pe.wait_ge(ot_ready, g * NC + c)
                for j in range(G):
                    last = nc.tensor.matmul(pv[j * VW:(j + 1) * VW, q0:BANK], vals[:, b, g * G + j, :],
                                            probs[:, (m + j // 2) % PRING, j % 2, 0:BANK - q0],
                                            start=(b == 0), stop=(b == (c + 1) * BANK // P - 1),
                                            tile_position=(0, j * VW))
                last.then_inc(pe_pv, 1)

            def turn_o(t):
                pe.wait_ge(ot_ready, NC * (NG - 1) + t // QT + 1)
                if t == 0:
                    pe.wait_ge(ring_read, len(USES))
                if t >= 2:
                    pe.wait_ge(lsum_read, t - 1)
                for g in range(NG):
                    last = nc.tensor.transpose(bank[t % 2][:, g * P:(g + 1) * P], o_t[:, g, t * P:(t + 1) * P], ident)
                last.then_inc(pe_ot, 1)

            def turn_mod(c):
                pe.wait_ge(mparts_ready, c + 1)
                if c >= 1:
                    pe.wait_ge(modt_ready, c)
                for t in range(QT):
                    last = nc.tensor.matmul(bank[2][0:KROWS, t * P:(t + 1) * P], mod_parts[:, c * QT + t, :, :],
                                            ident_b[:, :], start=True, stop=True)
                last.then_inc(pe_modt, 1)

            pe.wait_ge(masks_ready, 2)
            for kind, n in ORDER:
                if kind == RING_USE:
                    use_ring(n)
                elif kind == PAIR:
                    if n == 0:
                        pe.wait_ge(pool_set, 2)
                        pe.wait_ge(vals_ready, 2 * NT)
                    score_pair(n)
                elif kind == PROJECT:
                    project_part(n)
                elif kind == VALUES:
                    values(n)
                else:
                    weigh(*divmod(n, NSTEP))
                    if 0 <= n - FIRST_TURN < QT:
                        turn_o(n - FIRST_TURN)

            def product(out, w_hi, w_lo, f, c, stop):
                cols, toks = slice(f * P, (f + 1) * P), slice(c * BANK, (c + 1) * BANK)
                passes = [(w_hi, u_hi), (w_lo, u_hi), (w_hi, u_lo)]
                for i in range(NI):
                    for k, (w, act) in enumerate(passes):
                        last = nc.tensor.matmul(out, w[:, i, cols], act[:, i, toks], start=(i == 0 and k == 0),
                                                stop=(stop and i == NI - 1 and k == len(passes) - 1))
                return last

            def gate_product(n):
                c, f = divmod(n, NF)
                if n >= 2:
                    pe.wait_ge(silu_ready, n - 1)
                product(b8[n % 2], w_in_hi, w_in_lo, f, c, False)
                pe.wait_ge(modt_ready, c + 1)
                nc.tensor.matmul(b8[n % 2], b_stack[:, f * P:(f + 1) * P], mod_t[:, c * BANK:(c + 1) * BANK],
                                 start=False, stop=True).then_inc(pe_gate, 1)

            def up_product(n):
                c, f = divmod(n, NF)
                if n == 2:
                    pe.wait_ge(ot_ready, NG * NC)
                if n >= 3:
                    pe.wait_ge(gated, n - 2)
                product(UP_BANKS[n % 3], w_up_hi, w_up_lo, f, c, True).then_inc(pe_up, 1)

            pe.wait_ge(wsplit_ready, 3)
            pe.wait_ge(b_stacked, 16 * SLOTS)
            pe.wait_ge(exp_ready, 2 * NG * NSTEP)
            up_product(0)
            turn_mod(0)
            turn_o(QT)
            turn_o(QT + 1)
            up_product(1)
            turn_o(QT + 2)
            turn_o(QT + 3)
            for n in range(NF * NC):
                gate_product(n)
                if n + 2 < NF * NC:
                    up_product(n + 2)
                if n == 2:
                    turn_mod(1)
            pe.wait_ge(wsplit_ready, 4)
            pe.wait_ge(modt_ready, NC)
            for t in range(NT):
                pe.wait_ge(hid_ready, (t // QT + 1) * NF)
                if t >= 3:
                    pe.wait_ge(y_ready, t - 2)
                toks = slice(t * P, (t + 1) * P)
                for f in range(NF):
                    for k, (part_h, w) in enumerate(((0, w_down_hi), (1, w_down_hi), (0, w_down_lo))):
                        last = nc.tensor.matmul(b8[4 + t % 3][:, 0:D], hidden[f][:, part_h, toks], w[:, f, :],
                                                start=(f == 0 and k == 0), stop=(f == NF - 1 and k == 2))
                last.then_inc(pe_down, 1)

        def read_pv(act, k):
            g, c = divmod(k, NC)
            done = g * NSTEP + sum(cc <= c for cc, _, _ in STEPS)
            act.wait_ge(pe_pv, done)
            nc.scalar.copy(o_t[:, g, c * BANK:(c + 1) * BANK], pv[:, :]).then_inc(ot_ready, 1)

        @block.scalar
        def _(act):
            def read_weights():
                for i in range(NI):
                    act.wait_ge(pe_spec, i + 1)
                    nc.scalar.copy(spec_w[:, i, :], b8[4 + i]).then_inc(spec_ready, 1)

            def read_output():
                act.wait_ge(pe_speco, 1)
                nc.scalar.copy(spec_o[:, :, :], b8[6].rearrange("p (n m) -> p n m", n=NI)).then_inc(speco_ready, 1)

            def read_m():
                act.wait_ge(pe_m, 1)
                nc.scalar.copy(m_sb[:, :, :], b8[7][:, 0:NI * R].rearrange("p (n r) -> p n r", n=NI)).then_inc(m_ready, 1)

            def normalize(t):
                if t >= 2:
                    act.wait_ge(pe_xt, t - 1)
                if t % QT == 0:
                    act.wait_ge(bias_ready, t // QT + 1)
                nc.scalar.activation(xn[:, t % 2, :], x_sb[:, t, :], ACT.Identity, bias=bias[:, t:t + 1],
                                     scale=rstd[:, t:t + 1]).then_inc(xn_ready, 1)

            def read_xt(t):
                act.wait_ge(pe_xt, t + 1)
                if t >= 2:
                    act.wait_ge(pe_qk, t - 1)
                nc.scalar.copy(xn_t[:, t % 2, :], PSUM_T[:, 0:D]).then_inc(xt_ready, 1)

            def square(t):
                act.wait_ge(pe_qk, t + 1)
                if t >= 2:
                    act.wait_ge(ss_ready, t - 1)
                nc.scalar.activation(sq[:, t % 2, :], PSUM_QK[t % 2], ACT.Square).then_inc(sq_ready, 1)

            def read_pt(t):
                act.wait_ge(pe_pt, t + 1)
                if t >= 2:
                    act.wait_ge(pe_y, t - 1)
                nc.scalar.copy(prod_t[:, t % 2, :], PSUM_PT[:, 0:D]).then_inc(pt_ready, 1)

            def read_ut(t):
                act.wait_ge(pe_ut, t + 1)
                nc.scalar.copy(u_t[:, :, t * P:(t + 1) * P],
                               PSUM_UT[:, 0:D].rearrange("p (n m) -> p n m", n=NI)).then_inc(ut_ready, 1)

            def first_part(n):
                hf, c, w = PROJECTIONS[n]
                act.wait_ge(pe_proj, n + 1)
                nc.scalar.copy(part[w][hf][:, 0, c * BANK:(c + 1) * BANK], b8[n % 4]).then_inc(part1, 1)

            for c in range(NC):
                act.wait_ge(var_ready, c + 1)
                nc.scalar.activation(std[:, c * QT:(c + 1) * QT], veps[:, c * QT:(c + 1) * QT], ACT.Sqrt)\
                    .then_inc(std_ready, 1)
                if c == 0:
                    read_weights()
                    normalize(0)
                    normalize(1)
                    read_xt(0)
            for n in range(NT + 4):
                if 0 <= n - 1 < NT:
                    act.wait_ge(ss_ready, n)
                    nc.scalar.activation(norm[:, (n - 1) % 2, :], ss[:, (n - 1) % 2, :], ACT.Sqrt)\
                        .then_inc(norm_ready, 1)
                if n + 1 < NT:
                    read_xt(n + 1)
                if n < NT:
                    square(n)
                if 0 <= n - 4 < NT:
                    read_ut(n - 4)
                if n + 2 < NT:
                    normalize(n + 2)
                if n == 0:
                    read_output()
                    read_m()
                if 0 <= n - 2 < NT:
                    read_pt(n - 2)
                if 0 <= n - 3 < NT:
                    act.wait_ge(var2_ready, n - 2)
                    nc.scalar.activation(stds2[:, (n - 3) % 2, :], vars2[:, (n - 3) % 2, :], ACT.Sqrt)\
                        .then_inc(std2_ready, 1)
                if n == 3:
                    act.wait_ge(pe_wu, 1)
                    act.wait_ge(ld_ln, 16)
                    for i in range(NI):
                        nc.scalar.activation(w_u[:, i, 0:D], b8[7][:, i * D:(i + 1) * D], ACT.Copy,
                                             scale=lnw[:, 0, i:i + 1]).then_inc(wu_ready, 1)
                        nc.scalar.activation(w_u[:, i, D:D + R], a_sb[:, i, :], ACT.Copy,
                                             scale=lnw[:, 1, i:i + 1]).then_inc(wu_ready, 1)
                if n == NT + 1:
                    first_part(0)
            for n in range(1, 2 * NC):
                first_part(n)

            def read_values(t):
                act.wait_ge(pe_vals, t + 1)
                nc.scalar.copy(vals[:, t, :, 0:R], VALUE_BANKS[t % 3][:, 0:D].rearrange("p (h r) -> p h r", h=H))\
                    .then_inc(vals_ready, 1)
                nc.scalar.copy(ha[:, t, :], VALUE_BANKS[t % 3][:, D:D + R]).then_inc(vals_ready, 1)

            def tanh(c):
                toks = slice(c * QT, (c + 1) * QT)
                act.wait_ge(attn_ready, (c + 1) * QT)
                nc.scalar.activation(tanh_a[:, toks, :], attn_a[:, toks, :], ACT.Tanh).then_inc(tanh_ready, 1)

            def read_modt(c):
                act.wait_ge(pe_modt, c + 1)
                nc.scalar.copy(mod_t[:, c * BANK:(c + 1) * BANK], bank[2][0:KROWS, :]).then_inc(modt_ready, 1)

            def high(n):
                c, f = divmod(n, NF)
                act.wait_ge(gated, n + 1)
                nc.scalar.copy(hidden[f][:, 0, c * BANK:(c + 1) * BANK], gate[:, n % 4, :]).then_inc(high_ready, 1)

            def weights_of_pair(m):
                act.wait_ge(pe_pair, m + 1)
                if m >= PRING:
                    act.wait_ge(pe_pv, (m - PRING) // 2 + 1)
                columns = BANK - STEPS[m // 2 % NSTEP][2]
                nc.scalar.activation(probs[:, m % PRING, :, 0:columns], pair[m % 2][:, :, 0:columns],
                                     ACT.Exp, scale=HD ** -0.5).then_inc(exp_ready, 1)

            for kind, n in ORDER:
                if kind == PROJECT:
                    first_part(n)
                elif kind == VALUES:
                    read_values(n)
                elif kind == PAIR:
                    weights_of_pair(n)
                    if n == 2 * NG * NSTEP - 2:
                        tanh(0)
                elif kind == WEIGH:
                    c, b, _ = STEPS[n % NSTEP]
                    if b == (c + 1) * BANK // P - 1:
                        read_pv(act, n // NSTEP * NC + c)
            read_modt(0)
            tanh(1)
            for n in range(NF * NC):
                act.wait_ge(pe_gate, n + 1)
                if n >= 4:
                    act.wait_ge(hid_ready, n - 3)
                nc.scalar.activation(gate[:, n % 4, :], b8[n % 2], ACT.Silu).then_inc(silu_ready, 1)
                if n >= 1:
                    high(n - 1)
                if n == 2:
                    read_modt(1)
            high(NF * NC - 1)

        @block.gpsimd
        def _(pool):
            nc.gpsimd.memset(k_stack[KROWS:KROWS + MROWS, :, :, :, :], -1.0).then_inc(pool_set, 1)
            pool.wait_ge(pool_set, 1)
            nc.gpsimd.memset(vals[:, :, :, R:VW], 1.0).then_inc(pool_set, 1)
            pool.wait_ge(ld_ln, 16)
            pool.wait_ge(ld_attn, 80)
            for w in (f_q, f_k):
                for i in range(NI):
                    nc.gpsimd.tensor_scalar(w[:, i, :], w[:, i, :], lnw[:, 0, i:i + 1], None, ALU.mult)\
                        .then_inc(scaled_attn, 1)
            for t in range(NT + 2):
                if t < NT - 1:
                    pool.wait_ge(kvn_ready, t + 1)
                    if t == 0:
                        nc.gpsimd.tensor_copy(kv_sum[:, 1, :], qkn[:, 0, D:2 * D]).then_inc(sum_ready, 1)
                    else:
                        pool.wait_ge(sum_ready, t)
                        nc.gpsimd.tensor_tensor(kv_sum[:, t + 1, :], kv_sum[:, t, :], qkn[:, t % 2, D:2 * D],
                                                ALU.add).then_inc(sum_ready, 1)
                if t >= 2:
                    k = t - 2
                    pool.wait_ge(u_ready, k + 1)
                    nc.gpsimd.tensor_scalar(h0[:, k % 2, :], x1[:, k % 2, :], mv2[:, k % 2, 0:1], scales[:, k % 2, 0:1],
                                            ALU.subtract, ALU.mult).then_inc(pool_done, 1)
                    pool.wait_ge(pool_done, k + 1)
                    nc.gpsimd.tensor_tensor(base[:, k, :], x1[:, k % 2, :], h0[:, k % 2, :], ALU.add)\
                        .then_inc(base_ready, 1)
            for n in range(2 * NI * NC):
                hf, c, w = PROJECTIONS[n]
                cols = slice(c * BANK, (c + 1) * BANK)
                pool.wait_ge(rest1, n + 1)
                pool.wait_ge(part2, n + 1)
                nc.gpsimd.tensor_tensor(part[w][hf][:, 2, cols], rest[:, n % 2, :], part[w][hf][:, 1, cols],
                                        ALU.subtract).then_inc(part3, 1)
            steps = Counted(pool_steps)
            pool.wait_ge(ld_b, 16)
            pool.wait_ge(pool_steps, steps.mark(nc.gpsimd.tensor_copy(b_parts[:, 0, :], b_sb)))
            pool.wait_ge(pool_steps, steps.mark(
                nc.gpsimd.tensor_tensor(b_rest, b_sb, b_parts[:, 0, :], ALU.subtract)))
            pool.wait_ge(pool_steps, steps.mark(nc.gpsimd.tensor_copy(b_parts[:, 1, :], b_rest)))
            nc.gpsimd.tensor_tensor(b_parts[:, 2, :], b_rest, b_parts[:, 1, :], ALU.subtract).then_inc(bparts_ready, 2)
            pool.wait_ge(ld_mlp, 48)
            for w in (w_in, w_up):
                for i in range(NI):
                    v = steps.mark(nc.gpsimd.tensor_scalar(w[:, i, :], w[:, i, :], lnw[:, 1, i:i + 1], None, ALU.mult))
            pool.wait_ge(pool_steps, v)
            for group, whole, high, low in ((0, w_in, w_in_hi, w_in_lo), (0, w_up, w_up_hi, w_up_lo),
                                            (1, u_t, u_hi, u_lo), (1, w_down, w_down_hi, w_down_lo)):
                pool.wait_ge(pe_pair, 2 * (group + 1) * NSTEP)
                pool.wait_ge(pool_steps, steps.mark(nc.gpsimd.tensor_copy(high[:, :, :], whole[:, :, :])))
                nc.gpsimd.tensor_tensor(low[:, :, :], whole[:, :, :], high[:, :, :].bitcast(F32), ALU.subtract)\
                    .then_inc(wsplit_ready, 1)

        @block.vector
        def _(dve):
            done = Counted(dve_done)

            def need(value):
                dve.wait_ge(dve_done, value)

            for c in range(NC):
                half = slice(c * QT, (c + 1) * QT)
                dve.wait_ge(ld_x[c], 16)
                for t in range(c * QT, (c + 1) * QT):
                    v = done.mark(nc.vector.bn_stats(stats[:, t, :], x_sb[:, t, :]))
                need(v)
                for t in range(c * QT, (c + 1) * QT):
                    v = done.mark(nc.vector.bn_aggr(mv[:, t, :], stats[:, t, :]))
                need(v)
                nc.vector.tensor_scalar(veps[:, half], mv[:, half, 1], LN_EPS, None, ALU.add).then_inc(var_ready, 1)
                dve.wait_ge(std_ready, c + 1)
                need(done.mark(nc.vector.reciprocal(rstd[:, half], std[:, half])))
                nc.vector.scalar_tensor_tensor(bias[:, half], mv[:, half, 0], -1.0, rstd[:, half], ALU.mult, ALU.mult)\
                    .then_inc(bias_ready, 1)

            def spread_m():
                dve.wait_ge(m_ready, 1)
                dve.wait_ge(ld_cst, 16)
                for j in range(NI):
                    ins = nc.vector.tensor_tensor(
                        m_block[:, j, :, :], m_sb[:, j, :].unsqueeze(1).broadcast_to([P, HPH, R]),
                        cst[:, C_BLOCK:C_BLOCK + HPH].unsqueeze(2).broadcast_to([P, HPH, R]), ALU.mult)
                ins.then_inc(mblock_ready, 1)

            def energy(t):
                dve.wait_ge(sq_ready, t + 1)
                nc.vector.tensor_reduce(
                    ss[:, t % 2, :], sq[:, t % 2, :].rearrange("p (h s) -> p h s", s=HD), AX.X, ALU.add)\
                    .then_inc(ss_ready, 1)

            def unit(t):
                dve.wait_ge(norm_ready, t + 1)
                need(done.mark(nc.vector.reciprocal(inv_norm[:, t % 2, :], norm[:, t % 2, :])))
                if t >= 2:
                    dve.wait_ge(pe_cum, 2 * (t - 2) + 1)
                    dve.wait_ge(sum_ready, t - 1)
                for half, made in ((1, kvn_ready), (0, qn_ready)):
                    nc.vector.tensor_tensor(
                        qkn[:, t % 2, half * D:(half + 1) * D].rearrange("p (h s) -> p h s", s=HD),
                        PSUM_QK[t % 2][:, half * D:(half + 1) * D].rearrange("p (h s) -> p h s", s=HD),
                        inv_norm[:, t % 2, half * H:(half + 1) * H].unsqueeze(2).broadcast_to([P, H, HD]),
                        ALU.mult).then_inc(made, 1)

            def multiply(t):
                dve.wait_ge(pe_cum, 2 * t + 1)
                dve.wait_ge(qn_ready, t + 1)
                if t >= 2:
                    dve.wait_ge(pe_pt, t - 1)
                q = qkn[:, t % 2, 0:D].rearrange("p (h a s) -> p h a s", a=2, s=HD // 2)
                c = PSUM_C[:, 0:D].rearrange("p (h a s) -> p h a s", a=2, s=HD // 2)
                o = prod[:, t % 2, :].rearrange("p (h a s) -> p h a s", a=2, s=HD // 2)
                v = done.mark(nc.vector.tensor_tensor(prod[:, t % 2, :], qkn[:, t % 2, 0:D], PSUM_C[:, 0:D], ALU.mult))
                for e in range(2):
                    w = done.mark(nc.vector.tensor_tensor(cross[:, t % 2, e, :, :], q[:, :, e, :], c[:, :, 1 - e, :],
                                                          ALU.mult))
                need(v)
                v = done.mark(nc.vector.tensor_tensor(o[:, :, 0, 1:], o[:, :, 0, 1:], o[:, :, 1, 1:], ALU.subtract))
                need(v)
                nc.vector.tensor_tensor(o[:, :, 1, 1:], cross[:, t % 2, 0, :, 1:], cross[:, t % 2, 1, :, 1:],
                                        ALU.add).then_inc(prod_ready, 1)

            def norms(t):
                p = t % 2
                dve.wait_ge(pe_y, t + 1)
                if t >= 2:
                    dve.wait_ge(base_ready, t - 1)
                nc.vector.tensor_tensor(x1[:, p, :], x_sb[:, t, :], PSUM_Y[:, 0:D], ALU.add).then_inc(x1_ready, 1)
                dve.wait_ge(x1_ready, t + 1)
                need(done.mark(nc.vector.bn_stats(stats2[:, p, :], x1[:, p, :])))
                need(done.mark(nc.vector.bn_aggr(mv2[:, p, :], stats2[:, p, :])))
                v = done.mark(nc.vector.tensor_scalar(vars2[:, p, 0:1], mv2[:, p, 1:2], LN_EPS, None, ALU.add))
                nc.vector.tensor_scalar(vars2[:, p, 1:2], mv2[:, p, 1:2], 1 + RMS_EPS, LN_EPS * RMS_EPS, ALU.mult,
                                        ALU.add).then_inc(var2_ready, 1)

            def norm_u(t):
                p = t % 2
                dve.wait_ge(std2_ready, t + 1)
                need(done.mark(nc.vector.reciprocal(scales[:, p, :], stds2[:, p, :])))
                if t >= 2:
                    dve.wait_ge(pe_ut, t - 1)
                nc.vector.tensor_scalar(u[:, p, :], x1[:, p, :], mv2[:, p, 0:1], scales[:, p, 1:2], ALU.subtract, ALU.mult)\
                    .then_inc(u_ready, 1)

            def other_parts(n):
                hf, c, w = PROJECTIONS[n]
                dve.wait_ge(part1, n + 1)
                if n >= 2:
                    dve.wait_ge(part3, n - 1)
                nc.vector.tensor_tensor(rest[:, n % 2, :], b8[n % 4], part[w][hf][:, 0, c * BANK:(c + 1) * BANK],
                                        ALU.subtract).then_inc(rest1, 1)
                dve.wait_ge(rest1, n + 1)
                nc.vector.tensor_copy(part[w][hf][:, 1, c * BANK:(c + 1) * BANK], rest[:, n % 2, :]).then_inc(part2, 1)

            for n in range(NT + 4):
                if 0 <= n - 1 < NT:
                    energy(n - 1)
                if 0 <= n - 2 < NT:
                    multiply(n - 2)
                if 0 <= n - 1 < NT:
                    unit(n - 1)
                if 0 <= n - 3 < NT:
                    norms(n - 3)
                if n == 1:
                    spread_m()
                if n == 5:
                    for dst, src in ((ident_b, ident), (later_b, cst[:, C_LATER:C_LATER + P])):
                        nc.vector.tensor_copy(dst[:, :], src).then_inc(masks_ready, 1)
                if 0 <= n - 3 < NT:
                    norm_u(n - 3)
                if n == NT + 2:
                    other_parts(0)

            for n in range(1, 2 * NC):
                other_parts(n)

            def maxima(use):
                u, n = USES[use]
                j, i, k, keys = CHUNKS[u % NC][n]
                dve.wait_ge(pe_ring, use + 1)
                if use >= RING:
                    dve.wait_ge(ring_read, use - RING + 1)
                mask = C_MASK + S - (i + 1) * P + k * BANK
                nc.vector.tensor_tensor_reduce(junk[:, use % RING, 0:keys], bank[use % RING][:, 0:keys],
                                               cst[:, mask:mask + keys], 1.0, LOWEST, ALU.add, ALU.max,
                                               mpart[:, u % 2, k, i % QT, j:j + 1]).then_inc(ring_read, 1)

            def split_max(u, use):
                p, full = u % 2, mpart[:, u % 2, 0, :, :]
                dve.wait_ge(ring_read, use + 1)
                if u >= 2:
                    dve.wait_ge(pe_ring, UNIT_READY[u - 2])
                if u % NC:
                    need(done.mark(nc.vector.tensor_tensor(full, full, mpart[:, p, 1, :, :], ALU.max)))
                need(done.mark(nc.vector.tensor_copy(mparts[:, p, :, 0, :], full)))
                need(done.mark(nc.vector.tensor_tensor(mrest[:, :, :], full, mparts[:, p, :, 0, :], ALU.subtract)))
                need(done.mark(nc.vector.tensor_copy(mparts[:, p, :, 1, :], mrest[:, :, :])))
                nc.vector.tensor_tensor(mparts[:, p, :, 2, :], mrest[:, :, :], mparts[:, p, :, 1, :], ALU.subtract)\
                    .then_inc(maxp_ready, 1)

            dve.wait_ge(ld_mask, 16)
            for kind, number in ORDER:
                if kind == PROJECT:
                    other_parts(number)
                if kind != RING_USE:
                    continue
                of, n = USES[number]
                if n is None:
                    dve.wait_ge(pe_ring, number + 1)
                    if of >= 2:
                        dve.wait_ge(max_landed[of - 2], 16)
                    nc.vector.tensor_copy(mrows[:, of % 2, :], bank[number % RING][0:MROWS * G, :])\
                        .then_inc(ring_read, 1)
                else:
                    maxima(number)
                    if n == len(CHUNKS[of % NC]) - 1:
                        split_max(of, number)

            def by_token(t):
                o = bank[t % 2][:, :].rearrange("p (h v) -> p h v", v=VW)
                dve.wait_ge(pe_ot, t + 1)
                need(done.mark(nc.vector.reciprocal(linv[:, t % 2, :], o[:, :, R])))
                nc.vector.tensor_tensor(onorm[:, t % 2, :, :], o[:, :, 0:R],
                                        linv[:, t % 2, :].unsqueeze(2).broadcast_to([P, H, R]), ALU.mult)\
                    .then_inc(lsum_read, 1)
                dve.wait_ge(lsum_read, t + 1)
                nc.vector.tensor_reduce(attn_a[:, t, :], onorm[:, t % 2, :, :].rearrange("p h r -> p r h"),
                                        AX.X, ALU.add).then_inc(attn_ready, 1)

            def modulate(c):
                toks = slice(c * QT, (c + 1) * QT)
                m, rest_m, parts = mod_h[:, toks, :], mod_rest[:, toks, :], mod_parts[:, toks, :, :]

                def spread_part(src, first, slots):
                    return done.mark(nc.vector.tensor_copy(parts[:, :, first:first + slots, :],
                                                           src.unsqueeze(2).broadcast_to([P, QT, slots, R])))

                dve.wait_ge(tanh_ready, c + 1)
                need(done.mark(nc.vector.scalar_tensor_tensor(m, tanh_a[:, toks, :], MOD_SCALE, ha[:, toks, :],
                                                              ALU.mult, ALU.mult)))
                need(spread_part(m, 0, 3))
                need(done.mark(nc.vector.tensor_tensor(rest_m, m, parts[:, :, 0, :], ALU.subtract)))
                need(spread_part(rest_m, 3, 2))
                nc.vector.tensor_tensor(parts[:, :, 5, :], rest_m, parts[:, :, 3, :], ALU.subtract)\
                    .then_inc(mparts_ready, 1)

            dve.wait_ge(vals_ready, 2 * NT)
            for c in range(NC):
                for t in range(c * QT, (c + 1) * QT):
                    by_token(t)
                modulate(c)

            def low(n):
                c, f = divmod(n, NF)
                toks = slice(c * BANK, (c + 1) * BANK)
                dve.wait_ge(high_ready, n + 1)
                nc.vector.tensor_tensor(hidden[f][:, 1, toks], gate[:, n % 4, :], hidden[f][:, 0, toks].bitcast(F32),
                                        ALU.subtract).then_inc(hid_ready, 1)

            for n in range(NF * NC):
                dve.wait_ge(silu_ready, n + 1)
                dve.wait_ge(pe_up, n + 1)
                nc.vector.tensor_tensor(gate[:, n % 4, :], gate[:, n % 4, :], UP_BANKS[n % 3], ALU.mult).then_inc(gated, 1)
                if n >= 1:
                    low(n - 1)
            low(NF * NC - 1)
            dve.wait_ge(base_ready, NT)
            for t in range(NT):
                dve.wait_ge(pe_down, t + 1)
                nc.vector.tensor_tensor(y_sb[:, t, :], b8[4 + t % 3][:, 0:D], base[:, t, :], ALU.add).then_inc(y_ready, 1)


def by_row_of_head(w):
    return np.asarray(w).reshape(NG, G, HD, D).transpose(3, 0, 2, 1).reshape(D, D)


def kernel(L0_attn_x, L0_attn_W_q, L0_attn_W_kv, L0_attn_W_o, L0_ffn_ln1_w, L0_ffn_ln2_w, L0_ffn_Wq, L0_ffn_Wk,
           L0_ffn_Wv, L0_ffn_Wo, L0_ffn_A, L0_ffn_B, L0_ffn_W_in_base, L0_ffn_W_up_base, L0_ffn_W_down):
    from concourse import bacc
    from concourse.bass_utils import run_bass_kernel_spmd

    nc = bacc.Bacc("TRN2", target_bir_lowering=False, num_devices=1)
    arrays = {
        "x": np.asarray(L0_attn_x).reshape(S, D),
        "wq": L0_attn_W_q,
        "wkv": L0_attn_W_kv,
        "wo_t": np.asarray(L0_attn_W_o).T,
        "ln": np.stack([np.asarray(w).reshape(NI, P) for w in (L0_ffn_ln1_w, L0_ffn_ln2_w)]).transpose(2, 0, 1),
        "fwq_t": by_row_of_head(L0_ffn_Wq),
        "fwk_t": by_row_of_head(L0_ffn_Wk),
        "fwv": L0_ffn_Wv,
        "fwo": L0_ffn_Wo,
        "a": L0_ffn_A,
        "b": L0_ffn_B,
        "win_t": np.asarray(L0_ffn_W_in_base).T,
        "wup_t": np.asarray(L0_ffn_W_up_base).T,
        "wdown_t": np.asarray(L0_ffn_W_down).T,
        "consts": constants(),
    }
    arrays = {f"in_{k}": np.ascontiguousarray(v) for k, v in arrays.items()}
    args = [nc.dram_tensor(k, v.shape, mybir.dt.from_np(v.dtype), kind="ExternalInput").ap() for k, v in arrays.items()]
    out = nc.dram_tensor("out", (S, D), F32, kind="ExternalOutput").ap()
    seq_preln_kernel(nc, *args, out)
    r = run_bass_kernel_spmd(nc, [arrays], core_ids=[0])
    return r.results[0]["out"].reshape(1, S, D)
```
